# Optimizing a Trainium2 kernel written in Bass

```python
import numpy as np
import jax
import jax.numpy as jnp

def _softmax(x, axis=-1):
    return jax.nn.softmax(x, axis=axis)

def _gelu(x):
    return jax.nn.gelu(x, approximate=True)

def _silu(x):
    return jax.nn.silu(x)

def _sigmoid(x):
    return jax.nn.sigmoid(x)

def _layernorm(x, axis=-1, eps=1e-05):
    m = jnp.mean(x, axis=axis, keepdims=True)
    v = jnp.var(x, axis=axis, keepdims=True)
    return (x - m) / jnp.sqrt(v + eps)

def _scatter_add(tgt, idx, src, axis=0):
    return tgt.at[idx].add(src)

def _segment_sum(src, seg, n):
    return jax.ops.segment_sum(src, seg, n)
kernel_name = 'mk_perceiver_d1_seqx_r4_402457'

def setup_inputs(seed: int=0):
    np.random.seed(seed)
    _w = jnp.asarray

    def _rec_inputs():
        import jax
        import jax.numpy as jnp
        _rk = jax.random.key(seed)
        x = -4.161e-06 + 1 * jax.random.normal(jax.random.fold_in(_rk, 1), (1, 128, 512), jnp.float32)
        _lenS = 128 - jax.random.randint(jax.random.fold_in(_rk, 7), (1,), 0, max(1, 128 // 4) + 1, jnp.int32)
        _lenS2 = 12544 - jax.random.randint(jax.random.fold_in(_rk, 8), (1,), 0, max(1, 12544 // 4) + 1, jnp.int32)
        _ctx_2048P = jax.random.normal(jax.random.fold_in(_rk, 11), (1, 16, 512), jnp.float32)
        _ctx_2048c = jax.random.dirichlet(jax.random.fold_in(_rk, 511), 0.3 * jnp.ones((16,), jnp.float32), (1, 12544))
        _ctx_2048t = jnp.einsum('bsk,bkd->bsd', _ctx_2048c, _ctx_2048P)
        _ctx_2048t = _ctx_2048t * jax.lax.rsqrt(jnp.mean(jnp.square(_ctx_2048t)) + 1e-12) * 0.953939
        ctx_2048 = -0.000192764 + 0.999654 * (_ctx_2048t + 0.3 * jax.random.normal(jax.random.fold_in(_rk, 611), (1, 12544, 512), jnp.float32))
        return (x, ctx_2048)
    x, ctx_2048 = _rec_inputs()

    def _L0_xattn_setup():
        import jax, jax.numpy as jnp
        import numpy as np
        FP8_MAX = 448.0
        EPS = 1e-05

        def _fp8_roundtrip(x):
            return x.astype(jnp.float8_e4m3fn).astype(jnp.float32)

        def _div_clamp_fp8(x, scale):
            y = jnp.clip(x.astype(jnp.float32) / scale, -FP8_MAX, FP8_MAX)
            y = y.astype(jnp.bfloat16).astype(jnp.float32)
            return _fp8_roundtrip(y)

        def _ln(x, w, b):
            mu = jnp.mean(x, axis=-1, keepdims=True)
            var = jnp.mean(jnp.square(x - mu), axis=-1, keepdims=True)
            return (x - mu) * jax.lax.rsqrt(var + EPS) * w + b

        def _fp8_linear_pertensor(x, wq, w_scale, in_scale):
            xq = _div_clamp_fp8(x, in_scale)
            return jnp.einsum('bsi,oi->bso', xq * in_scale, wq) * w_scale

        def _gqa(q, k, v):
            scale = 1.0 / np.sqrt(q.shape[-1])
            scores = jnp.einsum('bsghd,btgd->bghst', q, k) * scale
            p = jax.nn.softmax(scores, axis=-1)
            return jnp.einsum('bghst,btgd->bsghd', p, v)
        key = jax.random.key(seed)
        ks = jax.random.split(key, 8)
        B, S, SC, H, NH, G, D = (2, 512, 128, 512, 16, 8, 128)

        def qw(k, out_f, in_f):
            w = jax.random.normal(k, (out_f, in_f), jnp.float32) * 0.02
            sc = jnp.max(jnp.abs(w)) / FP8_MAX
            return (_fp8_roundtrip(w / sc), sc.astype(jnp.float32))
        wq, wq_s = qw(ks[0], NH * D, H)
        wqx, wqx_s = qw(ks[1], NH * D, H)
        wk, wk_s = qw(ks[2], G * D, H)
        wv, wv_s = qw(ks[3], G * D, H)
        wproj, wp_s = qw(ks[4], H, 2 * NH * D)
        return {'hidden_states': jax.random.normal(ks[5], (B, S, H), jnp.float32), 'cond': jax.random.normal(ks[6], (B, SC, H), jnp.float32), 'ln_w': jnp.ones((H,), jnp.float32), 'ln_b': jnp.zeros((H,), jnp.float32), 'wq': wq, 'wq_scale': wq_s, 'q_in_scale': jnp.full((H,), 0.05, jnp.float32), 'wqx': wqx, 'wqx_scale': wqx_s, 'qx_in_scale': jnp.full((H,), 0.05, jnp.float32), 'wk': wk, 'wk_scale': wk_s, 'k_in_scale': jnp.full((H,), 0.05, jnp.float32), 'wv': wv, 'wv_scale': wv_s, 'v_in_scale': jnp.full((H,), 0.05, jnp.float32), 'w_kv_x': jax.random.normal(ks[7], (2 * G * D, H), jnp.float32) * 0.02, 'qln_w': jnp.ones((D,), jnp.float32), 'qln_b': jnp.zeros((D,), jnp.float32), 'kln_w': jnp.ones((D,), jnp.float32), 'kln_b': jnp.zeros((D,), jnp.float32), 'qxln_w': jnp.ones((D,), jnp.float32), 'qxln_b': jnp.zeros((D,), jnp.float32), 'kxln_w': jnp.ones((D,), jnp.float32), 'kxln_b': jnp.zeros((D,), jnp.float32), 'wproj': wproj, 'proj_w_scale': wp_s, 'proj_in_scale': jnp.asarray(0.05, jnp.float32), 'proj_smooth': jnp.full((2 * NH * D,), 0.05, jnp.float32)}
    _L0_xattn_all = _L0_xattn_setup()
    _L0_xattn_in = {k: v for k, v in _L0_xattn_all.items() if k in ('ln_w', 'ln_b', 'wq', 'wq_scale', 'q_in_scale', 'wqx', 'wqx_scale', 'qx_in_scale', 'wk', 'wk_scale', 'k_in_scale', 'wv', 'wv_scale', 'v_in_scale', 'w_kv_x', 'qln_w', 'qln_b', 'kln_w', 'kln_b', 'qxln_w', 'qxln_b', 'kxln_w', 'kxln_b', 'wproj', 'proj_w_scale', 'proj_in_scale', 'proj_smooth')}
    del _L0_xattn_all

    def _L0_attn_setup():
        import jax, jax.numpy as jnp
        import numpy as np
        D_MODEL = 512
        N_HEADS = 16
        D_HEAD = D_MODEL // N_HEADS
        B, S = (2, 512)
        EPS = 1e-05

        def _mhsa(X, ln_g, ln_b, Wq, bq, Wk, bk, Wv, bv, Wo, bo):
            n_ctx = X.shape[-2]
            mu = jnp.mean(X, axis=-1, keepdims=True)
            var = jnp.mean(jnp.square(X - mu), axis=-1, keepdims=True)
            Xn = (X - mu) * jax.lax.rsqrt(var + EPS) * ln_g + ln_b

            def split_heads(t):
                return t.reshape(t.shape[:-1] + (N_HEADS, D_HEAD)).swapaxes(-2, -3)
            Q = split_heads(Xn @ Wq + bq)
            K = split_heads(Xn @ Wk + bk)
            V = split_heads(Xn @ Wv + bv)
            scores = jnp.einsum('bhqd,bhkd->bhqk', Q, K) / jnp.sqrt(jnp.float32(D_HEAD))
            causal = jnp.tril(jnp.ones((n_ctx, n_ctx), dtype=bool))
            scores = jnp.where(causal, scores, jnp.float32(-jnp.inf))
            A = jax.nn.softmax(scores, axis=-1)
            AV = jnp.einsum('bhqk,bhkd->bhqd', A, V)
            AV = AV.swapaxes(-2, -3).reshape(X.shape[:-1] + (D_MODEL,))
            return AV @ Wo + bo
        key = jax.random.key(seed)
        ks = jax.random.split(key, 10)
        sd = 1.0 / np.sqrt(D_MODEL)
        inp = {'X': jax.random.normal(ks[0], (B, S, D_MODEL), dtype=jnp.float32), 'ln_g': jnp.ones((D_MODEL,), jnp.float32), 'ln_b': jnp.zeros((D_MODEL,), jnp.float32), 'Wq': jax.random.uniform(ks[1], (D_MODEL, D_MODEL), jnp.float32, -sd, sd), 'bq': jax.random.uniform(ks[2], (D_MODEL,), jnp.float32, -sd, sd), 'Wk': jax.random.uniform(ks[3], (D_MODEL, D_MODEL), jnp.float32, -sd, sd), 'bk': jax.random.uniform(ks[4], (D_MODEL,), jnp.float32, -sd, sd), 'Wv': jax.random.uniform(ks[5], (D_MODEL, D_MODEL), jnp.float32, -sd, sd), 'bv': jax.random.uniform(ks[6], (D_MODEL,), jnp.float32, -sd, sd), 'Wo': jax.random.uniform(ks[7], (D_MODEL, D_MODEL), jnp.float32, -sd, sd), 'bo': jax.random.uniform(ks[8], (D_MODEL,), jnp.float32, -sd, sd)}
        return inp
    _L0_attn_all = _L0_attn_setup()
    _L0_attn_in = {k: v for k, v in _L0_attn_all.items() if k in ('ln_g', 'ln_b', 'Wq', 'bq', 'Wk', 'bk', 'Wv', 'bv', 'Wo', 'bo')}
    del _L0_attn_all

    def _L0_ffn_setup():
        import jax, jax.numpy as jnp
        import numpy as np
        E = 32
        K = 8
        H = 512
        F = 192
        B, S = (1, 256)

        def _moe(x, wg, w1, v1, w2):
            T = x.shape[0]
            logits = x @ wg.T
            scores = jax.nn.softmax(logits, axis=-1)
            weights, idx = jax.lax.top_k(scores, K)
            weights = weights / jnp.sum(weights, axis=-1, keepdims=True)
            flat_e = idx.reshape(-1)
            flat_t = jnp.repeat(jnp.arange(T), K)
            flat_w = weights.reshape(-1)
            order = jnp.argsort(flat_e)
            e_s = flat_e[order]
            t_s = flat_t[order]
            w_s = flat_w[order]
            group_sizes = jnp.bincount(e_s, length=E).astype(jnp.int32)
            xs = x[t_s]
            g = jax.lax.ragged_dot(xs, w1, group_sizes)
            u = jax.lax.ragged_dot(xs, v1, group_sizes)
            h = jax.nn.silu(g) * u
            ys = jax.lax.ragged_dot(h, w2, group_sizes)
            out = jnp.zeros((T, x.shape[1]), x.dtype).at[t_s].add(ys * w_s[:, None])
            return out
        key = jax.random.key(seed)
        k0, k1, k2, k3, k4 = jax.random.split(key, 5)
        scale = 0.02
        return {'hidden_states': jax.random.normal(k0, (B, S, H), jnp.float32), 'wg': jax.random.normal(k1, (E, H), jnp.float32) * scale, 'w1': jax.random.normal(k2, (E, H, F), jnp.float32) * scale, 'v1': jax.random.normal(k3, (E, H, F), jnp.float32) * scale, 'w2': jax.random.normal(k4, (E, F, H), jnp.float32) * scale}
    _L0_ffn_all = _L0_ffn_setup()
    _L0_ffn_in = {k: v for k, v in _L0_ffn_all.items() if k in ('wg', 'w1', 'v1', 'w2')}
    del _L0_ffn_all
    return {'x': x, 'ctx_2048': ctx_2048, 'L0_xattn_ln_w': _L0_xattn_in['ln_w'], 'L0_xattn_ln_b': _L0_xattn_in['ln_b'], 'L0_xattn_wq': _L0_xattn_in['wq'], 'L0_xattn_wq_scale': _L0_xattn_in['wq_scale'], 'L0_xattn_q_in_scale': _L0_xattn_in['q_in_scale'], 'L0_xattn_wqx': _L0_xattn_in['wqx'], 'L0_xattn_wqx_scale': _L0_xattn_in['wqx_scale'], 'L0_xattn_qx_in_scale': _L0_xattn_in['qx_in_scale'], 'L0_xattn_wk': _L0_xattn_in['wk'], 'L0_xattn_wk_scale': _L0_xattn_in['wk_scale'], 'L0_xattn_k_in_scale': _L0_xattn_in['k_in_scale'], 'L0_xattn_wv': _L0_xattn_in['wv'], 'L0_xattn_wv_scale': _L0_xattn_in['wv_scale'], 'L0_xattn_v_in_scale': _L0_xattn_in['v_in_scale'], 'L0_xattn_w_kv_x': _L0_xattn_in['w_kv_x'], 'L0_xattn_qln_w': _L0_xattn_in['qln_w'], 'L0_xattn_qln_b': _L0_xattn_in['qln_b'], 'L0_xattn_kln_w': _L0_xattn_in['kln_w'], 'L0_xattn_kln_b': _L0_xattn_in['kln_b'], 'L0_xattn_qxln_w': _L0_xattn_in['qxln_w'], 'L0_xattn_qxln_b': _L0_xattn_in['qxln_b'], 'L0_xattn_kxln_w': _L0_xattn_in['kxln_w'], 'L0_xattn_kxln_b': _L0_xattn_in['kxln_b'], 'L0_xattn_wproj': _L0_xattn_in['wproj'], 'L0_xattn_proj_w_scale': _L0_xattn_in['proj_w_scale'], 'L0_xattn_proj_in_scale': _L0_xattn_in['proj_in_scale'], 'L0_xattn_proj_smooth': _L0_xattn_in['proj_smooth'], 'L0_attn_ln_g': _L0_attn_in['ln_g'], 'L0_attn_ln_b': _L0_attn_in['ln_b'], 'L0_attn_Wq': _L0_attn_in['Wq'], 'L0_attn_bq': _L0_attn_in['bq'], 'L0_attn_Wk': _L0_attn_in['Wk'], 'L0_attn_bk': _L0_attn_in['bk'], 'L0_attn_Wv': _L0_attn_in['Wv'], 'L0_attn_bv': _L0_attn_in['bv'], 'L0_attn_Wo': _L0_attn_in['Wo'], 'L0_attn_bo': _L0_attn_in['bo'], 'L0_ffn_wg': _L0_ffn_in['wg'], 'L0_ffn_w1': _L0_ffn_in['w1'], 'L0_ffn_v1': _L0_ffn_in['v1'], 'L0_ffn_w2': _L0_ffn_in['w2']}

def reference(x, ctx_2048, L0_xattn_ln_w, L0_xattn_ln_b, L0_xattn_wq, L0_xattn_wq_scale, L0_xattn_q_in_scale, L0_xattn_wqx, L0_xattn_wqx_scale, L0_xattn_qx_in_scale, L0_xattn_wk, L0_xattn_wk_scale, L0_xattn_k_in_scale, L0_xattn_wv, L0_xattn_wv_scale, L0_xattn_v_in_scale, L0_xattn_w_kv_x, L0_xattn_qln_w, L0_xattn_qln_b, L0_xattn_kln_w, L0_xattn_kln_b, L0_xattn_qxln_w, L0_xattn_qxln_b, L0_xattn_kxln_w, L0_xattn_kxln_b, L0_xattn_wproj, L0_xattn_proj_w_scale, L0_xattn_proj_in_scale, L0_xattn_proj_smooth, L0_attn_ln_g, L0_attn_ln_b, L0_attn_Wq, L0_attn_bq, L0_attn_Wk, L0_attn_bk, L0_attn_Wv, L0_attn_bv, L0_attn_Wo, L0_attn_bo, L0_ffn_wg, L0_ffn_w1, L0_ffn_v1, L0_ffn_w2):
    import jax
    import jax.numpy as jnp

    def _L0_xattn_ref(hidden_states, cond, ln_w, ln_b, wq, wq_scale, q_in_scale, wqx, wqx_scale, qx_in_scale, wk, wk_scale, k_in_scale, wv, wv_scale, v_in_scale, w_kv_x, qln_w, qln_b, kln_w, kln_b, qxln_w, qxln_b, kxln_w, kxln_b, wproj, proj_w_scale, proj_in_scale, proj_smooth):
        import jax, jax.numpy as jnp
        import numpy as np
        FP8_MAX = 448.0
        EPS = 1e-05

        def _fp8_roundtrip(x):
            return x.astype(jnp.float8_e4m3fn).astype(jnp.float32)

        def _div_clamp_fp8(x, scale):
            y = jnp.clip(x.astype(jnp.float32) / scale, -FP8_MAX, FP8_MAX)
            y = y.astype(jnp.bfloat16).astype(jnp.float32)
            return _fp8_roundtrip(y)

        def _ln(x, w, b):
            mu = jnp.mean(x, axis=-1, keepdims=True)
            var = jnp.mean(jnp.square(x - mu), axis=-1, keepdims=True)
            return (x - mu) * jax.lax.rsqrt(var + EPS) * w + b

        def _fp8_linear_pertensor(x, wq, w_scale, in_scale):
            xq = _div_clamp_fp8(x, in_scale)
            return jnp.einsum('bsi,oi->bso', xq * in_scale, wq) * w_scale

        def _gqa(q, k, v):
            scale = 1.0 / np.sqrt(q.shape[-1])
            scores = jnp.einsum('bsghd,btgd->bghst', q, k) * scale
            p = jax.nn.softmax(scores, axis=-1)
            return jnp.einsum('bghst,btgd->bsghd', p, v)
        b, s, _ = hidden_states.shape
        sc = cond.shape[1]
        d = qln_w.shape[0]
        nh = wq.shape[0] // d
        g = wk.shape[0] // d
        hpg = nh // g
        ln_out = _ln(hidden_states, ln_w, ln_b)
        q = _fp8_linear_pertensor(ln_out, wq, wq_scale, q_in_scale).reshape(b, s, g, hpg, d)
        q = _ln(q, qln_w, qln_b)
        k = _fp8_linear_pertensor(ln_out, wk, wk_scale, k_in_scale).reshape(b, s, g, d)
        k = _ln(k, kln_w, kln_b)
        v = _fp8_linear_pertensor(ln_out, wv, wv_scale, v_in_scale).reshape(b, s, g, d)
        core = _gqa(q, k, v).reshape(b, s, nh * d)
        qx = _fp8_linear_pertensor(ln_out, wqx, wqx_scale, qx_in_scale).reshape(b, s, g, hpg, d)
        qx = _ln(qx, qxln_w, qxln_b)
        kvx = jnp.einsum('bsi,oi->bso', cond, w_kv_x)
        kx, vx = jnp.split(kvx, 2, axis=-1)
        kx = _ln(kx.reshape(b, sc, g, d), kxln_w, kxln_b)
        vx = vx.reshape(b, sc, g, d)
        xout = _gqa(qx, kx, vx).reshape(b, s, nh * d)
        cat = jnp.concatenate([core, xout], axis=-1)
        catq = _div_clamp_fp8(cat, proj_smooth)
        return jnp.einsum('bsi,oi->bso', catq, wproj) * (proj_in_scale * proj_w_scale)

    def _L0_attn_ref(X, ln_g, ln_b, Wq, bq, Wk, bk, Wv, bv, Wo, bo):
        import jax, jax.numpy as jnp
        import numpy as np
        D_MODEL = 512
        N_HEADS = 16
        D_HEAD = D_MODEL // N_HEADS
        B, S = (2, 512)
        EPS = 1e-05

        def _mhsa(X, ln_g, ln_b, Wq, bq, Wk, bk, Wv, bv, Wo, bo):
            n_ctx = X.shape[-2]
            mu = jnp.mean(X, axis=-1, keepdims=True)
            var = jnp.mean(jnp.square(X - mu), axis=-1, keepdims=True)
            Xn = (X - mu) * jax.lax.rsqrt(var + EPS) * ln_g + ln_b

            def split_heads(t):
                return t.reshape(t.shape[:-1] + (N_HEADS, D_HEAD)).swapaxes(-2, -3)
            Q = split_heads(Xn @ Wq + bq)
            K = split_heads(Xn @ Wk + bk)
            V = split_heads(Xn @ Wv + bv)
            scores = jnp.einsum('bhqd,bhkd->bhqk', Q, K) / jnp.sqrt(jnp.float32(D_HEAD))
            causal = jnp.tril(jnp.ones((n_ctx, n_ctx), dtype=bool))
            scores = jnp.where(causal, scores, jnp.float32(-jnp.inf))
            A = jax.nn.softmax(scores, axis=-1)
            AV = jnp.einsum('bhqk,bhkd->bhqd', A, V)
            AV = AV.swapaxes(-2, -3).reshape(X.shape[:-1] + (D_MODEL,))
            return AV @ Wo + bo
        return _mhsa(X, ln_g, ln_b, Wq, bq, Wk, bk, Wv, bv, Wo, bo)

    def _L0_ffn_ref(hidden_states, wg, w1, v1, w2):
        import jax, jax.numpy as jnp
        import numpy as np
        E = 32
        K = 8
        H = 512
        F = 192
        B, S = (1, 256)

        def _moe(x, wg, w1, v1, w2):
            T = x.shape[0]
            logits = x @ wg.T
            scores = jax.nn.softmax(logits, axis=-1)
            weights, idx = jax.lax.top_k(scores, K)
            weights = weights / jnp.sum(weights, axis=-1, keepdims=True)
            flat_e = idx.reshape(-1)
            flat_t = jnp.repeat(jnp.arange(T), K)
            flat_w = weights.reshape(-1)
            order = jnp.argsort(flat_e)
            e_s = flat_e[order]
            t_s = flat_t[order]
            w_s = flat_w[order]
            group_sizes = jnp.bincount(e_s, length=E).astype(jnp.int32)
            xs = x[t_s]
            g = jax.lax.ragged_dot(xs, w1, group_sizes)
            u = jax.lax.ragged_dot(xs, v1, group_sizes)
            h = jax.nn.silu(g) * u
            ys = jax.lax.ragged_dot(h, w2, group_sizes)
            out = jnp.zeros((T, x.shape[1]), x.dtype).at[t_s].add(ys * w_s[:, None])
            return out
        Bb, Ss, Hh = hidden_states.shape
        x = hidden_states.reshape(Bb * Ss, Hh)
        out = _moe(x, wg, w1, v1, w2)
        return out.reshape(Bb, Ss, Hh)
    x = x + _L0_xattn_ref(_layernorm(x, axis=-1), ctx_2048, L0_xattn_ln_w, L0_xattn_ln_b, L0_xattn_wq, L0_xattn_wq_scale, L0_xattn_q_in_scale, L0_xattn_wqx, L0_xattn_wqx_scale, L0_xattn_qx_in_scale, L0_xattn_wk, L0_xattn_wk_scale, L0_xattn_k_in_scale, L0_xattn_wv, L0_xattn_wv_scale, L0_xattn_v_in_scale, L0_xattn_w_kv_x, L0_xattn_qln_w, L0_xattn_qln_b, L0_xattn_kln_w, L0_xattn_kln_b, L0_xattn_qxln_w, L0_xattn_qxln_b, L0_xattn_kxln_w, L0_xattn_kxln_b, L0_xattn_wproj, L0_xattn_proj_w_scale, L0_xattn_proj_in_scale, L0_xattn_proj_smooth)
    x = x + _L0_attn_ref(_layernorm(x, axis=-1), L0_attn_ln_g, L0_attn_ln_b, L0_attn_Wq, L0_attn_bq, L0_attn_Wk, L0_attn_bk, L0_attn_Wv, L0_attn_bv, L0_attn_Wo, L0_attn_bo)
    x = x + _L0_ffn_ref(_layernorm(x, axis=-1), L0_ffn_wg, L0_ffn_w1, L0_ffn_v1, L0_ffn_w2)
    return x

_drawn_inputs = setup_inputs


def setup_inputs(seed=0):
    import zlib

    import numpy as np

    out = dict(_drawn_inputs(seed))
    spreads = {'L0_xattn_ln_w': (1.0, 0.2),
     'L0_xattn_ln_b': (0.0, 0.1),
     'L0_xattn_q_in_scale': (0.05000000074505806, 0.6),
     'L0_xattn_qx_in_scale': (0.05000000074505806, 0.6),
     'L0_xattn_k_in_scale': (0.05000000074505806, 0.6),
     'L0_xattn_v_in_scale': (0.05000000074505806, 0.6),
     'L0_xattn_qln_w': (1.0, 0.6),
     'L0_xattn_qln_b': (0.0, 0.8),
     'L0_xattn_kln_w': (1.0, 0.6),
     'L0_xattn_kln_b': (0.0, 0.8),
     'L0_xattn_qxln_w': (1.0, 0.6),
     'L0_xattn_qxln_b': (0.0, 0.685),
     'L0_xattn_kxln_w': (1.0, 0.6),
     'L0_xattn_kxln_b': (0.0, 0.1),
     'L0_xattn_proj_smooth': (0.05000000074505806, 0.2),
     'L0_attn_ln_g': (1.0, 0.6),
     'L0_attn_ln_b': (0.0, 0.1)}
    factors = {'L0_attn_Wq': 2.763,
     'L0_attn_bq': 8.0,
     'L0_attn_Wk': 2.777,
     'L0_attn_bk': 8.0,
     'L0_attn_bv': 3.907,
     'L0_ffn_wg': 4.224,
     'L0_ffn_w1': 3.413,
     'L0_ffn_v1': 3.34,
     'L0_ffn_w2': 3.301}
    for name, (base, spread) in spreads.items():
        noise = np.random.default_rng([zlib.crc32(name.encode()), seed]).standard_normal(out[name].shape)
        drawn = base * np.exp(spread * noise) if base else spread * noise
        out[name] = jnp.asarray(drawn.astype(out[name].dtype))
    for name, factor in factors.items():
        out[name] = (out[name] * factor).astype(out[name].dtype)
    return out
```

```python
from contextlib import ExitStack

import concourse.bass as bass
from concourse import mybir

ALU = mybir.AluOpType
ACT = mybir.ActivationFunctionType
AX = mybir.AxisListType.X
F32 = mybir.dt.float32
F16 = mybir.dt.float16
BF16 = mybir.dt.bfloat16
I32 = mybir.dt.int32

P = 128
T = 128
C = 512
NC = C // P
D = 128
NH = 16
G = 8
HPG = NH // G
S_CTX = 12544
TILES = 7
BLK = TILES * P
NBLK = S_CTX // BLK
HALF = BLK // 2
EPS = 1e-5
FP8_MAX = 448.0
W_UP = 256.0
V_UP = 16.0
Q_UP = 16.0
P_UP = 4096.0
UNITS = [(0, 1), (2, 3), (4, 5), (6,)]
TURNS = [(0, 4), (4, 7)]
SH = 16
SD = C // SH
E = 32
K_TOP = 8
F = 192
SLOTS = 8
BIG = 1e30

COLS = {}
_at = 0
for _name, _n in (("q_in", NC), ("qx_in", NC), ("k_in", NC), ("v_in", NC), ("smooth", 2 * NH),
                  ("ln_w", NC), ("ln_b", NC), ("qln_w", 1), ("qln_b", 1), ("kln_w", 1), ("kln_b", 1),
                  ("qxln_w", 1), ("qxln_b", 1), ("kxln_w", 1), ("kxln_b", 1),
                  ("ln_g2", NC), ("ln_b2", NC), ("bq", NC), ("bk", NC)):
    COLS[_name] = (_at, _at + _n)
    _at += _n
N_COLS = _at
SCALARS = ("wq", "wqx", "wk", "wv", "proj_w", "proj_in")
ROWS = 2 * C + len(SCALARS)


def build(nc, x, ctxT, wqT, wqxT, wkT, wvT, wkvT, wprojT, cols_in, rows_in, Wq, Wk, Wv, Wo, wgT, w1v1, w2, out):
    with ExitStack() as ctx:
        named = {}

        def sem(name):
            if name not in named:
                named[name] = ctx.enter_context(nc.semaphore(name))
            return named[name]

        base0 = nc.sbuf_base
        limit = nc.sbuf_usable_end
        size = {F32: 4, F16: 2, BF16: 2, I32: 4}

        class Place:
            def __init__(self, at):
                self.at = at

            def put(self, name, shape, dt):
                n = size[dt]
                for k in shape[1:]:
                    n *= k
                t = nc.alloc_sbuf_tensor_at(name, shape, dt, offset=self.at)
                self.at += (n + 31) // 32 * 32
                assert self.at <= limit, (name, self.at, limit)
                return t

        small = Place((base0 + 31) // 32 * 32)
        ident = small.put("ident", [P, P], F32)
        causal = small.put("causal", [P, P], F32)
        cols = small.put("cols", [P, N_COLS], F32)
        rcp_in = small.put("rcp_in", [P, 4 * NC + 2 * NH], F32)
        rows = small.put("rows", [P, ROWS], F32)
        neghalf = small.put("neghalf", [P, NH], F32)
        stat = small.put("stat", [P, NH, 6], F32)
        mv = small.put("mv", [P, NH, 2], F32)
        vare = small.put("vare", [P, NH], F32)
        rstd = small.put("rstd", [P, NH], F32)
        mx = small.put("mx", [P, NH], F32)
        nmx = small.put("nmx", [P, NH], F32)
        den = small.put("den", [P, NH], F32)
        rden = small.put("rden", [P, NH], F32)
        pscale = small.put("pscale", [P, 1], F32)
        kstat = small.put("kstat", [P, 2, 2, 6], F32)
        kmv = small.put("kmv", [P, 2, 2, 2], F32)
        kvar = small.put("kvar", [P, 2, 2], F32)
        krstd = small.put("krstd", [P, 2, 2], F32)
        bmax = small.put("bmax", [P, NH], F32)
        k_eps = small.put("k_eps", [P, 2], F32)
        nm_new = small.put("nm_new", [P, NH], F32)
        nm_old = small.put("nm_old", [P, NH], F32)
        alpha = small.put("alpha", [P, NH], F32)
        rsum = small.put("rsum", [P, NH], F32)
        lsum = small.put("lsum", [P, NH], F32)
        xs = small.put("xs", [P, C], F32)
        slot_x = Place(small.at)

        def expert_slot(place, k):
            return (place.put(f"w1v1_{k}", [P, NC, 2 * F], F32), place.put(f"w2a_{k}", [P, C], F32),
                    place.put(f"w2b_{k}", [P, C], F32))

        b0 = slot_x.at
        pb = Place(b0)
        wq_s = pb.put("wq_s", [P, NC, NH * D], F32)
        wk_s = pb.put("wk_s", [P, NC, G * D], F32)
        wv_s = pb.put("wv_s", [P, NC, G * D], F32)
        b1 = pb.at
        pb = Place(b0)
        k_sb = pb.put("k_sb", [P, G * D], F32)
        v_sb = pb.put("v_sb", [P, G * D], F32)
        khatT = pb.put("khatT", [P, G * D], F32)
        probs = pb.put("probs", [P, NH, T], F32)
        probsT = pb.put("probsT", [P, NH, T], F32)
        pb = Place(b0 + NC * NH * D * 4)
        wkv_s = pb.put("wkv_s", [P, NC, 2 * G * D], F32)
        wproj_s = Place(b0).put("wproj_s", [P, 2 * NH, C], F32)
        pb = Place(b0)
        slots_b = [expert_slot(pb, k) for k in range(3, 9)]
        assert pb.at <= b1

        m0 = b1
        pm = Place(m0)
        coreq = pm.put("coreq", [P, NH, T], F32)
        w_hl = pm.put("w_hl", [P, 2, NC, G, 2 * D], F16)
        ctx_s = pm.put("ctx_s", [P, NC, BLK], F32)
        qx_hl = pm.put("qx_hl", [P, 2, NH, T], F16)
        m1 = pm.at
        ctx_hl = pm.put("ctx_hl", [P, 2, NC, BLK], F16)
        kn = pm.put("kn", [P, 2, BLK], F32)
        khT = pm.put("khT", [P, 2, 2, BLK], F16)
        vhl = pm.put("vhl", [P, 4, 2, BLK], F16)
        kfull = pm.put("kfull", [P, BLK], F32)
        pr = pm.put("pr", [P, 2, BLK], F32)
        prT = pm.put("prT", [P, 2, 2, BLK], F16)
        acc = pm.put("acc", [P, NH, D], F32)
        pa = Place(m1)
        wqx_s = pa.put("wqx_s", [P, NC, NH * D], F32)
        y_bf = pa.put("y_bf", [P, 4 * NC, T], BF16)
        y_f = pa.put("y_f", [P, 4 * NC, T], F32)
        y_c = pa.put("y_c", [P, 4 * NC, T], F32)
        q_sb = pa.put("q_sb", [P, NH, D], F32)
        qT = pa.put("qT", [P, NH, T], F32)
        xq = y_c
        lnT = pa.put("lnT", [P, NC, T], F32)
        xn = pa.put("xn", [P, C], F32)
        pd = Place(m0 + NH * T * 4)
        sw = [pd.put(f"sw{k}", [P, NC, C], F32) for k in range(4)]
        assert pd.at <= m0 + NH * T * 4 + 32768
        pd = Place(m1)
        xoutq = pd.put("xoutq", [P, NH, T], F32)
        z_f = pd.put("z_f", [P, NH, T], F32)
        z_c = pd.put("z_c", [P, NH, T], F32)
        z_bf = pd.put("z_bf", [P, NH, T], BF16)
        assert pd.at <= m1 + (2 * NC * BLK * 2 + 2 * BLK * 4 + 4 * BLK * 2 + 8 * BLK * 2)
        slots_a = [expert_slot(Place(m0 + NH * T * 4 + 32768), 0)]
        pd = Place(m1 + (2 * NC * BLK * 2 + 2 * BLK * 4 + 4 * BLK * 2 + 8 * BLK * 2))
        a_xn = pd.put("a_xn", [P, C], F32)
        a_xT = pd.put("a_xT", [P, NC, T], F32)
        a_QT = pd.put("a_QT", [P, NC, T], F32)
        a_KT = pd.put("a_KT", [P, NC, T], F32)
        a_V = pd.put("a_V", [P, C], F32)
        a_o = pd.put("a_o", [P, C], F32)
        a_oT = pd.put("a_oT", [P, NC, T], F32)
        wg_s = pd.put("wg_s", [P, NC, E], F32)
        gate = pd.put("gate", [P, E], F32)
        gate2 = pd.put("gate2", [P, E], F32)
        top8 = pd.put("top8", [P, K_TOP], F32)
        silu = pd.put("silu", [P, 2, F], F32)
        hid = pd.put("hid", [P, 2, F], F32)
        hidT = pd.put("hidT", [P, 2, 2, T], F32)
        ysum = pd.put("ysum", [P, C], F32)
        pd = Place(m1)
        a_P = pd.put("a_P", [P, 4, NC, T], F32)
        a_PT = pd.put("a_PT", [P, SH, T], F32)
        slots_c = [expert_slot(Place(pd.at), 1)]
        slots = (slots_a + slots_c + slots_b)[:SLOTS]
        SLOT_AFTER = ["context", "context", "proj", "proj", "proj", "proj", "proj", "proj"]

        ps = ctx.enter_context(nc.psum_tensor("ps", [P, 8, 512], F32))
        KV, TT, SS, OO = 0, 2, 5, 7

        def col(name, k=0):
            return cols[:, COLS[name][0] + k:COLS[name][0] + k + 1]

        def scalar(name):
            k = 2 * C + SCALARS.index(name)
            return rows[:, k:k + 1]

        def count(b, g, per_step, k):
            return b * (G * per_step) + (g * per_step + k)

        block = ctx.enter_context(nc.Block())

        @block.sync
        def _(sp):
            sp.dma_start(xs[:, :], x).then_inc(sem("x_in"), 16)
            sp.dma_start(cols[:, :], cols_in).then_inc(sem("cols_in"), 16)
            sp.dma_start(rows[:, :], rows_in.partition_broadcast(P)).then_inc(sem("rows_in"), 16)
            sp.dma_start(wk_s[:, :, :], wkT.rearrange("(c p) n -> p c n", p=P)).then_inc(sem("wk_in"), 16)
            sp.dma_start(wv_s[:, :, :], wvT.rearrange("(c p) n -> p c n", p=P)).then_inc(sem("wv_in"), 16)
            sp.dma_start(wq_s[:, :, :], wqT.rearrange("(c p) n -> p c n", p=P)).then_inc(sem("wq_in"), 16)
            sp.dma_start(wqx_s[:, :, :], wqxT.rearrange("(c p) n -> p c n", p=P)).then_inc(sem("wqx_in"), 16)
            ctx_view = ctxT.rearrange("(c p) t -> p c t", p=P)
            sp.dma_start(ctx_s[:, :, :], ctx_view[:, :, 0:BLK]).then_inc(sem("ctx_in"), 16)
            sp.wait_ge(sem("kproj_mm"), 2)
            sp.wait_ge(sem("vproj_mm"), 2)
            sp.dma_start(wkv_s[:, :, :], wkvT.rearrange("(c p) n -> p c n", p=P)).then_inc(sem("wkv_in"), 16)
            sp.wait_ge(sem("own_pv_mm"), 4)
            sp.wait_ge(sem("wkv_lo"), NC)
            sp.dma_start(wproj_s[:, :, :], wprojT.rearrange("(c p) n -> p c n", p=P)).then_inc(sem("wproj_in"), 16)
            with sp.Fori(0, NBLK - 1) as b:
                sp.wait_ge(sem("ctx_split"), b * TILES + TILES)
                sp.dma_start(ctx_s[:, :, :], ctx_view[:, :, bass.ds(b * BLK + BLK, BLK)]).then_inc(sem("ctx_in"), 16)

            def load_expert(slot, e):
                w13, wa, wb = slots[slot]
                s = sem(f"expert_in{slot}")
                sp.dma_start(w13[:, :, :], w1v1[e].rearrange("(c p) f -> p c f", p=P)).then_inc(s, 16)
                sp.dma_start(wa[:, :], w2[e][0:P, :]).then_inc(s, 16)
                sp.dma_start(wb[0:F - P, :], w2[e][P:F, :]).then_inc(s, 16)

            sp.wait_ge(sem("kv_mm"), NBLK * G * len(UNITS))
            for k, w in enumerate((Wq, Wk, Wv, Wo)):
                sp.dma_start(sw[k][:, :, :], w.rearrange("(c p) n -> p c n", p=P)).then_inc(sem(f"sw{k}_in"), 16)
            load_expert(0, 0)
            sp.wait_ge(sem("o_done"), NBLK * NH + 1)
            sp.dma_start(wg_s[:, :, :], wgT.rearrange("(c p) n -> p c n", p=P)).then_inc(sem("wg_in"), 16)
            sp.wait_ge(sem("proj_mm"), 1)
            for slot in range(1, SLOTS):
                load_expert(slot, slot)
            with sp.Fori(0, E // SLOTS - 1) as it:
                for slot in range(SLOTS):
                    sp.wait_ge(sem("y_mm"), it * SLOTS + (slot + 1))
                    w13, wa, wb = slots[slot]
                    e = it * SLOTS + (SLOTS + slot)
                    s = sem(f"expert_in{slot}")
                    sp.dma_start(w13[:, :, :], w1v1.rearrange("e (c p) f -> p (e c) f", p=P)[:, bass.ds(e * NC, NC), :]).then_inc(s, 16)
                    sp.dma_start(wa[:, :], w2[bass.ds(e, 1), 0:P, :].rearrange("o f n -> (o f) n")).then_inc(s, 16)
                    sp.dma_start(wb[0:F - P, :], w2[bass.ds(e, 1), P:F, :].rearrange("o f n -> (o f) n")).then_inc(s, 16)
            sp.wait_ge(sem("final"), 1)
            sp.dma_start(out, xs[:, :]).then_inc(sem("out_done"), 16)
            sp.wait_ge(sem("out_done"), 16)

        @block.tensor
        def _(pe):
            def transposes(dst_bank, src, n, signal, group=4):
                for k in range(n):
                    mm = pe.transpose(ps[:, dst_bank + k // group, (k % group) * P:(k % group + 1) * P], src(k), ident[:, :])
                    if k % group == group - 1 or k == n - 1:
                        mm.then_inc(sem(signal), 1)

            def project(bank, xT, w, n_blocks, signal):
                for n in range(n_blocks):
                    for c in range(NC):
                        mm = pe.matmul(ps[:, bank + n, :], xT[:, c, :], w[:, c, n * 512:(n + 1) * 512],
                                       start=(c == 0), stop=(c == NC - 1))
                    mm.then_inc(sem(signal), 1)

            pe.wait_ge(sem("ident"), 1)
            pe.wait_ge(sem("xn2"), 1)
            transposes(0, lambda k: xn[:, k * P:(k + 1) * P], NC, "xnT_mm")
            pe.wait_ge(sem("xq"), 1)
            pe.wait_ge(sem("wk_in"), 16)
            project(0, xq[:, 2 * NC:3 * NC, :], wk_s, 2, "kproj_mm")
            pe.wait_ge(sem("wv_in"), 16)
            project(2, xq[:, 3 * NC:4 * NC, :], wv_s, 2, "vproj_mm")
            pe.wait_ge(sem("wq_in"), 16)
            project(4, xq[:, 0:NC, :], wq_s, 4, "qproj_mm")
            pe.wait_ge(sem("k_sb"), 2)
            pe.wait_ge(sem("v_sb"), 2)
            pe.wait_ge(sem("wqx_in"), 16)
            project(0, xq[:, NC:2 * NC, :], wqx_s, 4, "qxproj_mm")
            pe.wait_ge(sem("q_sb"), 4)
            pe.wait_ge(sem("kn_own"), 1)
            transposes(4, lambda k: k_sb[:, k * P:(k + 1) * P], G, "khatT_mm")
            pe.wait_ge(sem("qn_own"), 1)
            pe.wait_ge(sem("qx_sb"), 4)
            transposes(0, lambda k: q_sb[:, k, :], NH, "qhatT_mm")
            pe.wait_ge(sem("khatT"), 2)
            pe.wait_ge(sem("qhatT"), 4)
            for h in range(NH):
                mm = pe.matmul(ps[:, 4 + h // 4, (h % 4) * T:(h % 4 + 1) * T], qT[:, h, :],
                               khatT[:, (h // HPG) * P:(h // HPG + 1) * P], start=True, stop=True)
            mm.then_inc(sem("own_scores_mm"), 1)
            pe.wait_ge(sem("qxn"), 1)
            transposes(0, lambda k: y_f[:, k, :], NH, "qxhatT_mm")
            pe.wait_ge(sem("own_probs"), NH)
            pe.wait_ge(sem("qxhatT"), 4)
            transposes(0, lambda k: probs[:, k, :], NH, "own_probsT_mm")
            pe.wait_ge(sem("own_probsT"), 4)
            for h in range(NH):
                mm = pe.matmul(ps[:, 4 + h // 4, (h % 4) * D:(h % 4 + 1) * D], probsT[:, h, :],
                               v_sb[:, (h // HPG) * D:(h // HPG + 1) * D], start=True, stop=True)
                if h % 4 == 3:
                    mm.then_inc(sem("own_pv_mm"), 1)
            pe.wait_ge(sem("core"), 1)
            transposes(0, lambda k: q_sb[:, k, :], NH, "coreT_mm")

            def kv_unit(b, g, u, in_block=None):
                if g == 0:
                    pe.wait_ge(sem("ctx_split"), b * TILES + (UNITS[u][-1] + 1))
                first = isinstance(b, int) and b == 0 and g == 0 and u < 2
                if not first:
                    pe.wait_ge(sem("v_hi"), count(b, g, 4, u - 1))
                    pe.wait_ge(sem("v_lo"), count(b, g, 4, u - 1))
                    pe.wait_ge(sem("k_norm"), count(b, g, 4, u - 1))
                for i, t in enumerate(UNITS[u]):
                    o = ps[:, KV + u % 2, i * 2 * D:(i + 1) * 2 * D]
                    for c in range(NC):
                        for xp, wp in ((0, 0), (0, 1), (1, 0)):
                            mm = pe.matmul(o, ctx_hl[:, xp, c, t * P:(t + 1) * P], w_hl[:, wp, c, g, :],
                                           start=(c == 0 and xp + wp == 0), stop=(c == NC - 1 and xp == 1))
                mm.then_inc(sem("kv_mm"), 1)

            def k_turn(b, g):
                pe.wait_ge(sem("k_norm"), count(b, g, 4, 4))
                for j, (t0, t1) in enumerate(TURNS):
                    for t in range(t0, t1):
                        mm = pe.transpose(ps[:, TT + j, (t - t0) * P:(t - t0 + 1) * P], kn[:, g % 2, t * P:(t + 1) * P], ident[:, :])
                    mm.then_inc(sem("k_turn_mm"), 1)

            def scores(b, g, h):
                head = g * HPG + h
                if h == 0:
                    pe.wait_ge(sem("k_hi"), count(b, g, 2, 2))
                    pe.wait_ge(sem("k_lo"), count(b, g, 2, 2))
                else:
                    pe.wait_ge(sem("probs"), count(b, g, 2, 1))
                for qp, kp in ((0, 0), (0, 1), (1, 0)):
                    for half in range(2):
                        mm = pe.matmul(ps[:, SS + half, 0:HALF], qx_hl[:, qp, head, :],
                                       khT[:, g % 2, kp, half * HALF:(half + 1) * HALF],
                                       start=(qp + kp == 0), stop=(qp == 1), skip_group_check=True)
                mm.then_inc(sem("scores_mm"), 1)

            def p_turn(b, g, h, turn_keys):
                pe.wait_ge(sem("probs"), count(b, g, 2, h + 1))
                for j, (t0, t1) in enumerate(TURNS):
                    bank = TT + (2 * (h + 1) + j) % 3
                    if turn_keys and (h, j) == (0, 1):
                        pe.wait_ge(sem("k_hi"), count(b, g + 1, 2, 1))
                        pe.wait_ge(sem("k_full"), count(b, g + 1, 2, 1))
                    if turn_keys and (h, j) == (1, 0):
                        pe.wait_ge(sem("k_hi"), count(b, g + 1, 2, 2))
                        pe.wait_ge(sem("k_full"), count(b, g + 1, 2, 2))
                    for t in range(t0, t1):
                        mm = pe.transpose(ps[:, bank, (t - t0) * P:(t - t0 + 1) * P], pr[:, h, t * P:(t + 1) * P], ident[:, :])
                    mm.then_inc(sem("p_turn_mm"), 1)

            def outputs(b, g, h):
                pe.wait_ge(sem("p_hi"), count(b, g, 4, 2 * h + 2))
                pe.wait_ge(sem("p_lo"), count(b, g, 4, 2 * h + 2))
                if h == 0:
                    pe.wait_ge(sem("v_hi"), count(b, g, 4, 4))
                    pe.wait_ge(sem("v_lo"), count(b, g, 4, 4))
                pe.wait_ge(sem("o_done"), count(b, g, 2, h + 1))
                for t in range(TILES):
                    for pp, vp in ((0, 0), (0, 1), (1, 0)):
                        mm = pe.matmul(ps[:, OO, 0:D], prT[:, h, pp, t * P:(t + 1) * P], vhl[:, g % 4, vp, t * P:(t + 1) * P],
                                       start=(t == 0 and pp + vp == 0), stop=(t == TILES - 1 and pp == 1))
                mm.then_inc(sem("pv_mm"), 1)

            def step(b, g, last):
                project_on = not (last and g >= G - 2)
                turn_on = not (last and g == G - 1)
                b2, g2 = (b, g + 2) if g + 2 < G else (b + 1, g + 2 - G)
                b1_, g1 = (b, g + 1) if g + 1 < G else (b + 1, 0)
                scores(b, g, 0)
                if project_on:
                    kv_unit(b2, g2, 0)
                if turn_on:
                    k_turn(b1_, g1)
                scores(b, g, 1)
                p_turn(b, g, 0, turn_on)
                if project_on:
                    kv_unit(b2, g2, 1)
                outputs(b, g, 0)
                p_turn(b, g, 1, turn_on)
                if project_on:
                    kv_unit(b2, g2, 2)
                outputs(b, g, 1)
                if project_on:
                    kv_unit(b2, g2, 3)

            pe.wait_ge(sem("wkv_hi"), NC)
            pe.wait_ge(sem("wkv_lo"), NC)
            pe.wait_ge(sem("coreT"), 2 * NH)
            for g in range(2):
                for u in range(len(UNITS)):
                    kv_unit(0, g, u)
            k_turn(0, 0)
            pe.wait_ge(sem("k_hi"), 2)
            pe.wait_ge(sem("k_full"), 2)
            pe.wait_ge(sem("qx_hl"), 2)
            with pe.Fori(0, NBLK - 1) as b:
                for g in range(G):
                    step(b, g, False)
            for g in range(G):
                step(NBLK - 1, g, True)

            pe.wait_ge(sem("xout"), 1)
            transposes(0, lambda k: acc[:, k, :], NH, "xoutT_mm")
            pe.wait_ge(sem("wproj_in"), 16)
            for c in range(NH):
                pe.matmul(ps[:, 4, :], coreq[:, c, :], wproj_s[:, c, :], start=(c == 0), stop=False)
            pe.wait_ge(sem("xoutq"), 1)
            for c in range(NH):
                mm = pe.matmul(ps[:, 4, :], xoutq[:, c, :], wproj_s[:, NH + c, :], start=False, stop=(c == NH - 1))
            mm.then_inc(sem("proj_mm"), 1)

            pe.wait_ge(sem("a_xn"), 1)
            transposes(0, lambda k: a_xn[:, k * P:(k + 1) * P], NC, "a_xT_mm")
            pe.wait_ge(sem("a_xT"), NC)
            for k, (w, signal) in enumerate(((0, "a_QT_mm"), (1, "a_KT_mm"))):
                pe.wait_ge(sem(f"sw{w}_in"), 16)
                for m in range(NC):
                    for c in range(NC):
                        mm = pe.matmul(ps[:, 1 + k, m * T:(m + 1) * T], sw[w][:, c, m * P:(m + 1) * P], a_xT[:, c, :],
                                       start=(c == 0), stop=(c == NC - 1))
                mm.then_inc(sem(signal), 1)
            pe.wait_ge(sem("sw2_in"), 16)
            project(3, a_xT, sw[2], 1, "a_V_mm")
            pe.wait_ge(sem("a_QT"), NC)
            pe.wait_ge(sem("a_KT"), NC)
            for j in range(4):
                for m in range(NC):
                    mm = pe.matmul(ps[:, 4 + j, m * T:(m + 1) * T], a_QT[j * SD:(j + 1) * SD, m, :],
                                   a_KT[j * SD:(j + 1) * SD, m, :], start=True, stop=True)
                mm.then_inc(sem("a_scores_mm"), 1)
            pe.wait_ge(sem("a_probs"), SH)
            pe.wait_ge(sem("a_V"), 1)
            transposes(0, lambda k: a_P[:, k // 4, k % 4, :], SH, "a_PT_mm")
            pe.wait_ge(sem("a_PT"), 4)
            for k in range(SH):
                head = (k % 4) * 4 + k // 4
                mm = pe.matmul(ps[:, 4, head * SD:(head + 1) * SD], a_PT[:, k, :], a_V[:, head * SD:(head + 1) * SD],
                               start=True, stop=True)
            mm.then_inc(sem("a_pv_mm"), 1)
            pe.wait_ge(sem("a_o"), 1)
            transposes(0, lambda k: a_o[:, k * P:(k + 1) * P], NC, "a_oT_mm")
            pe.wait_ge(sem("a_oT"), 1)
            pe.wait_ge(sem("sw3_in"), 16)
            project(5, a_oT, sw[3], 1, "a_out_mm")

            pe.wait_ge(sem("e_xn"), 1)
            transposes(0, lambda k: a_xn[:, k * P:(k + 1) * P], NC, "e_xT_mm")
            pe.wait_ge(sem("e_xT"), 1)
            pe.wait_ge(sem("wg_in"), 16)
            for c in range(NC):
                mm = pe.matmul(ps[:, 1, 0:E], a_xT[:, c, :], wg_s[:, c, :], start=(c == 0), stop=(c == NC - 1))
            mm.then_inc(sem("logits_mm"), 1)
            pe.wait_ge(sem("gate"), 1)

            with pe.Fori(0, E // SLOTS) as it:
                def up(k):
                    pe.wait_ge(sem(f"expert_in{k}"), it * 48 + 48)
                    if k >= 2:
                        pe.wait_ge(sem("hid"), it * SLOTS + (k - 1))
                    for c in range(NC):
                        mm = pe.matmul(ps[:, 2 + k % 2, 0:2 * F], a_xT[:, c, :], slots[k][0][:, c, :],
                                       start=(c == 0), stop=(c == NC - 1))
                    mm.then_inc(sem("up_mm"), 1)

                def turn(k):
                    pe.wait_ge(sem("hid"), it * SLOTS + (k + 1))
                    if k >= 2:
                        pe.wait_ge(sem("hidT"), it * (2 * SLOTS) + (2 * k - 2))
                    pe.transpose(ps[:, 4 + k % 2, 0:T], hid[:, k % 2, 0:P], ident[:, :])
                    pe.transpose(ps[0:F - P, 4 + k % 2, T:2 * T], hid[:, k % 2, P:F], ident[:, :]).then_inc(sem("hid_turn_mm"), 1)

                def down(k):
                    pe.wait_ge(sem("hidT"), it * (2 * SLOTS) + (2 * k + 2))
                    pe.matmul(ps[:, 6, :], hidT[:, k % 2, 0, :], slots[k][1][:, :], start=(k == 0), stop=False)
                    pe.matmul(ps[:, 6, :], hidT[0:F - P, k % 2, 1, :], slots[k][2][0:F - P, :], start=False,
                              stop=(k == SLOTS - 1)).then_inc(sem("y_mm"), 1)

                pe.wait_ge(sem("ysum"), it * 1 + 1)
                up(0)
                for k in range(SLOTS):
                    if k + 1 < SLOTS:
                        up(k + 1)
                    turn(k)
                    if k:
                        down(k - 1)
                down(SLOTS - 1)

        @block.scalar
        def _(act):
            act.wait_ge(sem("rows_in"), 16)
            for n in range(2):
                act.wait_ge(sem("kproj_mm"), n + 1)
                if n == 0:
                    act.wait_ge(sem("qproj_mm"), 4)
                act.activation(k_sb[:, n * 512:(n + 1) * 512], ps[:, n, :], ACT.Copy, scale=scalar("wk")).then_inc(sem("k_sb"), 1)
            for n in range(2):
                act.wait_ge(sem("vproj_mm"), n + 1)
                act.activation(v_sb[:, n * 512:(n + 1) * 512], ps[:, 2 + n, :], ACT.Copy, scale=scalar("wv")).then_inc(sem("v_sb"), 1)
            for n in range(4):
                act.wait_ge(sem("qproj_mm"), n + 1)
                act.activation(q_sb[:, 4 * n:4 * n + 4, :], ps[:, 4 + n, :].rearrange("p (a d) -> p a d", d=D), ACT.Copy,
                               scale=scalar("wq")).then_inc(sem("q_sb"), 1)
            for n in range(4):
                act.wait_ge(sem("qxproj_mm"), n + 1)
                act.activation(y_f[:, 4 * n:4 * n + 4, :], ps[:, n, :].rearrange("p (a d) -> p a d", d=D), ACT.Copy,
                               scale=scalar("wqx")).then_inc(sem("qx_sb"), 1)
            for n in range(2):
                act.wait_ge(sem("khatT_mm"), n + 1)
                act.activation(khatT[:, n * 512:(n + 1) * 512], ps[:, 4 + n, :], ACT.Identity, bias=col("kln_b"),
                               scale=col("kln_w")).then_inc(sem("khatT"), 1)
            for n in range(4):
                act.wait_ge(sem("qhatT_mm"), n + 1)
                act.activation(qT[:, 4 * n:4 * n + 4, :], ps[:, n, :].rearrange("p (a d) -> p a d", d=D), ACT.Identity,
                               bias=col("qln_b"), scale=col("qln_w")).then_inc(sem("qhatT"), 1)
            act.wait_ge(sem("own_nmax"), 1)
            for h in range(NH):
                act.activation(probs[:, h, :], ps[:, 4 + h // 4, (h % 4) * T:(h % 4 + 1) * T], ACT.Exp, bias=nmx[:, h:h + 1],
                               scale=D ** -0.5, accum_out=den[:, h:h + 1]).then_inc(sem("own_probs"), 1)
            for n in range(4):
                act.wait_ge(sem("own_probsT_mm"), n + 1)
                act.activation(probsT[:, 4 * n:4 * n + 4, :], ps[:, n, :].rearrange("p (a d) -> p a d", d=D), ACT.Copy)\
                   .then_inc(sem("own_probsT"), 1)
            act.wait_ge(sem("wkv_in"), 16)
            for c in range(NC):
                act.activation(w_hl[:, 0, c, :, :], wkv_s[:, c, :].rearrange("p (g n) -> p g n", g=G), ACT.Copy, scale=W_UP)\
                   .then_inc(sem("wkv_hi"), 1)

            def v_high(b, g, u):
                act.wait_ge(sem("kv_mm"), count(b, g, 4, u + 1))
                n, t0 = len(UNITS[u]), UNITS[u][0]
                act.activation(vhl[:, g % 4, 0, t0 * P:(t0 + n) * P].rearrange("p (t d) -> p t d", d=D),
                               ps[:, KV + u % 2, 0:n * 2 * D].rearrange("p (t k d) -> p t k d", k=2, d=D)[:, :, 1, :], ACT.Copy,
                               scale=V_UP / W_UP).then_inc(sem("v_hi"), 1)

            def ctx_high(b, t):
                if t == 0:
                    act.wait_ge(sem("ctx_in"), b * 16 + 16)
                sl = slice(t * P, (t + 1) * P)
                act.activation(ctx_hl[:, 0, :, sl], ctx_s[:, :, sl], ACT.Copy).then_inc(sem("ctx_high"), 1)

            def k_affine(b, g, first=False):
                for j, (t0, t1) in enumerate(TURNS):
                    src = ps[:, TT + j, 0:(t1 - t0) * P]
                    act.wait_ge(sem("k_turn_mm"), count(b, g, 2, j + 1))
                    act.activation(khT[:, g % 2, 0, t0 * P:t1 * P], src, ACT.Identity, bias=col("kxln_b"),
                                   scale=col("kxln_w")).then_inc(sem("k_hi"), 1)
                    if not first:
                        act.wait_ge(sem("k_lo"), count(b, g, 2, j - 1))
                    act.activation(kfull[:, t0 * P:t1 * P], src, ACT.Identity, bias=col("kxln_b"),
                                   scale=col("kxln_w")).then_inc(sem("k_full"), 1)

            def exps(b, g, h):
                head = g * HPG + h
                act.wait_ge(sem("nm_new"), count(b, g, 2, h + 1))
                act.activation(pr[:, h, :].rearrange("p (a n) -> p a n", a=2), ps[:, SS:SS + 2, 0:HALF], ACT.Exp,
                               bias=nm_new[:, head:head + 1], scale=1.0 / Q_UP,
                               accum_out=rsum[:, head:head + 1]).then_inc(sem("probs"), 1)
                act.activation(alpha[:, head:head + 1], nm_old[:, head:head + 1], ACT.Exp, bias=nm_new[:, head:head + 1],
                               scale=-1.0).then_inc(sem("alpha"), 1)

            def p_high(b, g, h):
                for j, (t0, t1) in enumerate(TURNS):
                    act.wait_ge(sem("p_turn_mm"), count(b, g, 4, 2 * h + j + 1))
                    act.activation(prT[:, h, 0, t0 * P:t1 * P], ps[:, TT + (2 * (h + 1) + j) % 3, 0:(t1 - t0) * P], ACT.Copy,
                                   scale=P_UP).then_inc(sem("p_hi"), 1)

            def step(b, g, last):
                project_on = not (last and g >= G - 2)
                turn_on = not (last and g == G - 1)
                b2, g2 = (b, g + 2) if g + 2 < G else (b + 1, g + 2 - G)
                b1_, g1 = (b, g + 1) if g + 1 < G else (b + 1, 0)
                split_on = g == G - 3 and not last

                def unit(u):
                    v_high(b2, g2, u)
                    if split_on:
                        for t in UNITS[u]:
                            ctx_high(b + 1, t)

                exps(b, g, 0)
                if project_on:
                    unit(0)
                if turn_on:
                    k_affine(b1_, g1)
                exps(b, g, 1)
                p_high(b, g, 0)
                if project_on:
                    unit(1)
                p_high(b, g, 1)
                if project_on:
                    unit(2)
                    unit(3)

            for t in range(TILES):
                ctx_high(0, t)
            for g in range(2):
                for u in range(len(UNITS)):
                    v_high(0, g, u)
            k_affine(0, 0, first=True)
            with act.Fori(0, NBLK - 1) as b:
                for g in range(G):
                    step(b, g, False)
            for g in range(G):
                step(NBLK - 1, g, True)

            act.wait_ge(sem("a_nmax"), 1)
            for k in range(SH):
                act.activation(a_P[:, k // 4, k % 4, :], a_P[:, k // 4, k % 4, :], ACT.Exp, bias=nmx[:, k:k + 1],
                               accum_out=den[:, k:k + 1]).then_inc(sem("a_probs"), 1)
            for n in range(4):
                act.wait_ge(sem("a_PT_mm"), n + 1)
                act.activation(a_PT[:, 4 * n:4 * n + 4, :], ps[:, n, :].rearrange("p (a d) -> p a d", d=T), ACT.Copy)\
                   .then_inc(sem("a_PT"), 1)
            act.wait_ge(sem("e_nmax"), 1)
            act.activation(gate[:, :], ps[:, 1, 0:E], ACT.Exp, bias=nmx[:, 0:1], accum_out=den[:, 0:1]).then_inc(sem("e_exp"), 1)
            with act.Fori(0, E // SLOTS) as it:
                for k in range(SLOTS):
                    act.wait_ge(sem("up_mm"), it * SLOTS + (k + 1))
                    if k >= 2:
                        act.wait_ge(sem("hid"), it * SLOTS + (k - 1))
                    act.activation(silu[:, k % 2, :], ps[:, 2 + k % 2, 0:F], ACT.Silu).then_inc(sem("silu"), 1)

        @block.gpsimd
        def _(pool):
            links = [0]

            def link(ins):
                links[0] += 1
                ins.then_inc(sem("pool_link"), 1)
                pool.wait_ge(sem("pool_link"), links[0])

            link(pool.memset(ident[:, :], 0.0))
            pool.affine_select(out=ident[:, :], in_=ident[:, :], compare_op=ALU.not_equal, fill=1.0, base=0,
                               pattern=[[-1, P]], channel_multiplier=1).then_inc(sem("ident"), 1)
            link(pool.memset(causal[:, :], 0.0))
            pool.affine_select(out=causal[:, :], in_=causal[:, :], compare_op=ALU.is_ge, fill=-BIG, base=0,
                               pattern=[[-1, P]], channel_multiplier=1).then_inc(sem("causal"), 1)
            link(pool.memset(neghalf[:, :], -0.5))
            link(pool.memset(k_eps[:, :], EPS * W_UP * W_UP))

            def rstds(tag, n):
                pool.wait_ge(sem(f"var_{tag}"), 1)
                link(pool.tensor_scalar(vare[:, 0:n], mv[:, 0:n, 1], EPS, 1.0, ALU.add, ALU.mult))
                pool.tensor_tensor(rstd[:, 0:n], vare[:, 0:n], neghalf[:, 0:n], ALU.pow).then_inc(sem(f"rstd_{tag}"), 1)

            rstds("x", 1)
            rstds("x1", 1)
            rstds("k_own", G)
            rstds("q_own", NH)
            rstds("qx", NH)

            def split_tile(b, t):
                sl = slice(t * P, (t + 1) * P)
                pool.wait_ge(sem("ctx_high"), b * TILES + (t + 1))
                pool.tensor_tensor(ctx_hl[:, 1, :, sl], ctx_s[:, :, sl], ctx_hl[:, 0, :, sl], ALU.subtract)\
                    .then_inc(sem("ctx_split"), 1)

            def k_rstd(b, g, u):
                n = len(UNITS[u])
                pool.wait_ge(sem("k_var"), count(b, g, 4, u + 1))
                pool.tensor_tensor(kvar[:, u % 2, 0:n], kmv[:, u % 2, 0:n, 1], k_eps[:, 0:n], ALU.add)\
                    .then_inc(sem("k_vare"), 1)
                pool.wait_ge(sem("k_vare"), count(b, g, 4, u + 1))
                pool.tensor_tensor(krstd[:, u % 2, 0:n], kvar[:, u % 2, 0:n], neghalf[:, 0:n], ALU.pow).then_inc(sem("k_rstd"), 1)

            def k_low(b, g):
                for j, (t0, t1) in enumerate(TURNS):
                    sl = slice(t0 * P, t1 * P)
                    pool.wait_ge(sem("k_full"), count(b, g, 2, j + 1))
                    pool.tensor_tensor(khT[:, g % 2, 1, sl], kfull[:, sl], khT[:, g % 2, 0, sl], ALU.subtract)\
                        .then_inc(sem("k_lo"), 1)

            def step(b, g, last):
                project_on = not (last and g >= G - 2)
                turn_on = not (last and g == G - 1)
                split_on = g == G - 3 and not last
                b2, g2 = (b, g + 2) if g + 2 < G else (b + 1, g + 2 - G)
                b1_, g1 = (b, g + 1) if g + 1 < G else (b + 1, 0)

                def split_unit(u):
                    if split_on:
                        for t in UNITS[u]:
                            split_tile(b + 1, t)

                if project_on:
                    k_rstd(b2, g2, 0)
                if turn_on:
                    k_low(b1_, g1)
                split_unit(0)
                for u in range(1, len(UNITS)):
                    if project_on:
                        k_rstd(b2, g2, u)
                    split_unit(u)

            for t in range(TILES):
                split_tile(0, t)
            for g in range(2):
                for u in range(len(UNITS)):
                    k_rstd(0, g, u)
            k_low(0, 0)
            with pool.Fori(0, NBLK - 1) as b:
                for g in range(G):
                    step(b, g, False)
            for g in range(G):
                step(NBLK - 1, g, True)
            for tag in ("a1", "a2", "e1"):
                rstds(tag, 1)

        @block.vector
        def _(dve):
            links = [0]

            def link(ins):
                links[0] += 1
                ins.then_inc(sem("dve_link"), 1)
                dve.wait_ge(sem("dve_link"), links[0])

            def norm_row(tag, dst, src, signal=None):
                link(dve.bn_stats(stat[:, 0, :], src))
                dve.bn_aggr(mv[:, 0, :], stat[:, 0, :]).then_inc(sem(f"var_{tag}"), 1)
                dve.wait_ge(sem(f"var_{tag}"), 1)
                dve.wait_ge(sem(f"rstd_{tag}"), 1)
                ins = dve.tensor_scalar(dst, src, mv[:, 0, 0:1], rstd[:, 0:1], ALU.subtract, ALU.mult)
                if signal:
                    ins.then_inc(sem(signal), 1)
                else:
                    link(ins)

            def norm_heads(tag, src, n, signal):
                for h in range(n):
                    ins = dve.bn_stats(stat[:, h, :], src(h))
                link(ins)
                for h in range(n):
                    ins = dve.bn_aggr(mv[:, h, :], stat[:, h, :])
                ins.then_inc(sem(f"var_{tag}"), 1)
                dve.wait_ge(sem(f"var_{tag}"), 1)
                dve.wait_ge(sem(f"rstd_{tag}"), 1)
                for h in range(n):
                    ins = dve.tensor_scalar(src(h), src(h), mv[:, h, 0:1], rstd[:, h:h + 1], ALU.subtract, ALU.mult)
                ins.then_inc(sem(signal), 1)

            def round_fp8(y_bf_, y_f_, y_c_):
                link(dve.tensor_copy(y_f_, y_bf_))
                link(dve.tensor_scalar(y_c_.bitcast(I32), y_f_.bitcast(I32), 0x7F800000, None, ALU.bitwise_and))
                link(dve.tensor_scalar(y_c_, y_c_, 2.0 ** -6, 1.5 * 2.0 ** 20, ALU.max, ALU.mult))
                link(dve.tensor_tensor(y_f_, y_f_, y_c_, ALU.add))
                return dve.tensor_tensor(y_f_, y_f_, y_c_, ALU.subtract)

            dve.wait_ge(sem("x_in"), 16)
            norm_row("x", xn[:, :], xs[:, :])
            norm_row("x1", xn[:, :], xn[:, :], "xn2")
            dve.wait_ge(sem("cols_in"), 16)
            link(dve.reciprocal(rcp_in[:, :], cols[:, 0:4 * NC + 2 * NH]))
            dve.wait_ge(sem("xnT_mm"), 1)
            for c in range(NC):
                ins = dve.tensor_scalar(lnT[:, c, :], ps[:, 0, c * T:(c + 1) * T], col("ln_w", c), col("ln_b", c), ALU.mult, ALU.add)
            link(ins)
            for k in range(4 * NC):
                ins = dve.tensor_scalar(y_c[:, k, :], lnT[:, k % NC, :], rcp_in[:, k:k + 1], FP8_MAX, ALU.mult, ALU.min)
            link(ins)
            link(dve.tensor_scalar(y_bf[:, :, :], y_c[:, :, :], -FP8_MAX, None, ALU.max))
            link(round_fp8(y_bf[:, :, :], y_f[:, :, :], y_c[:, :, :]))
            for k in range(4 * NC):
                ins = dve.tensor_scalar(xq[:, k, :], y_f[:, k, :], cols[:, k:k + 1], None, ALU.mult)
            ins.then_inc(sem("xq"), 1)
            dve.wait_ge(sem("k_sb"), 2)
            norm_heads("k_own", lambda h: k_sb[:, h * D:(h + 1) * D], G, "kn_own")
            dve.wait_ge(sem("q_sb"), 4)
            norm_heads("q_own", lambda h: q_sb[:, h, :], NH, "qn_own")
            dve.wait_ge(sem("qx_sb"), 4)
            norm_heads("qx", lambda h: y_f[:, h, :], NH, "qxn")
            dve.wait_ge(sem("own_scores_mm"), 1)
            link(dve.tensor_reduce(mx[:, :].rearrange("p (a b) -> p a b", a=4),
                                   ps[:, 4:8, :].rearrange("p a (b n) -> p a b n", b=4), AX, ALU.max))
            dve.tensor_scalar(nmx[:, :], mx[:, :], -D ** -0.5, None, ALU.mult).then_inc(sem("own_nmax"), 1)
            for n in range(4):
                dve.wait_ge(sem("qxhatT_mm"), n + 1)
                ins = dve.tensor_scalar(y_c[:, 4 * n:4 * n + 4, :], ps[:, n, :].rearrange("p (a d) -> p a d", d=D), col("qxln_w"),
                                        col("qxln_b"), ALU.mult, ALU.add)
                ins.then_inc(sem("qxhatT"), 1)
            dve.wait_ge(sem("qxhatT"), 4)
            link(dve.tensor_scalar(y_c[:, :, :], y_c[:, :, :], Q_UP * D ** -0.5, None, ALU.mult))
            dve.tensor_copy(qx_hl[:, 0, :, :], y_c[:, :, :]).then_inc(sem("qx_hl"), 1)
            dve.wait_ge(sem("qx_hl"), 1)
            dve.tensor_tensor(qx_hl[:, 1, :, :], y_c[:, :, :], qx_hl[:, 0, :, :], ALU.subtract).then_inc(sem("qx_hl"), 1)
            for c in range(NC):
                dve.wait_ge(sem("wkv_hi"), c + 1)
                dve.scalar_tensor_tensor(out=w_hl[:, 1, c, :, :].rearrange("p g n -> p (g n)"), in0=wkv_s[:, c, :], scalar=W_UP,
                                         in1=w_hl[:, 0, c, :, :].rearrange("p g n -> p (g n)"), op0=ALU.mult,
                                         op1=ALU.subtract).then_inc(sem("wkv_lo"), 1)
            dve.wait_ge(sem("own_probs"), NH)
            link(dve.reciprocal(rden[:, :], den[:, :]))
            for h in range(NH):
                dve.wait_ge(sem("own_pv_mm"), h // 4 + 1)
                ins = dve.tensor_scalar(q_sb[:, h, :], ps[:, 4 + h // 4, (h % 4) * D:(h % 4 + 1) * D], rden[:, h:h + 1], None, ALU.mult)
            ins.then_inc(sem("core"), 1)
            for h in range(NH):
                dve.wait_ge(sem("coreT_mm"), h // 4 + 1)
                dve.tensor_scalar(y_c[:, h, :], ps[:, h // 4, (h % 4) * T:(h % 4 + 1) * T], rcp_in[:, 4 * NC + h:4 * NC + h + 1],
                                  FP8_MAX, ALU.mult, ALU.min).then_inc(sem("coreT"), 1)
            dve.wait_ge(sem("coreT"), NH)
            link(dve.tensor_scalar(y_bf[:, :, :], y_c[:, :, :], -FP8_MAX, None, ALU.max))
            link(round_fp8(y_bf[:, :, :], y_f[:, :, :], y_c[:, :, :]))
            dve.tensor_copy(coreq[:, :, :], y_f[:, :, :]).then_inc(sem("coreT"), NH)
            dve.wait_ge(sem("coreT"), 2 * NH)
            dve.memset(nm_old[:, :], BIG)
            dve.memset(lsum[:, :], 0.0)
            dve.memset(acc[:, :, :], 0.0).then_inc(sem("o_done"), 1)
            dve.wait_ge(sem("o_done"), 1)

            def unit_out(b, g, u):
                n, t0 = len(UNITS[u]), UNITS[u][0]
                bank = ps[:, KV + u % 2, :]
                dve.wait_ge(sem("v_hi"), count(b, g, 4, u + 1))
                for i in range(n):
                    ins = dve.bn_stats(kstat[:, u % 2, i, :], bank[:, i * 2 * D:i * 2 * D + D])
                ins.then_inc(sem("k_stat"), 1)
                dve.wait_ge(sem("k_stat"), count(b, g, 4, u + 1))
                dve.scalar_tensor_tensor(
                    out=vhl[:, g % 4, 1, t0 * P:(t0 + n) * P].rearrange("p (t d) -> p t d", d=D),
                    in0=bank[:, 0:n * 2 * D].rearrange("p (t k d) -> p t k d", k=2, d=D)[:, :, 1, :], scalar=V_UP / W_UP,
                    in1=vhl[:, g % 4, 0, t0 * P:(t0 + n) * P].rearrange("p (t d) -> p t d", d=D),
                    op0=ALU.mult, op1=ALU.subtract).then_inc(sem("v_lo"), 1)
                for i in range(n):
                    ins = dve.bn_aggr(kmv[:, u % 2, i, :], kstat[:, u % 2, i, :])
                ins.then_inc(sem("k_var"), 1)

            def unit_norm(b, g, u):
                dve.wait_ge(sem("k_rstd"), count(b, g, 4, u + 1))
                dve.wait_ge(sem("k_var"), count(b, g, 4, u + 1))
                for i, t in enumerate(UNITS[u]):
                    ins = dve.tensor_scalar(kn[:, g % 2, t * P:(t + 1) * P], ps[:, KV + u % 2, i * 2 * D:i * 2 * D + D],
                                            kmv[:, u % 2, i, 0:1], krstd[:, u % 2, i:i + 1], ALU.subtract, ALU.mult)
                ins.then_inc(sem("k_norm"), 1)

            def row_max(b, g, h):
                head = g * HPG + h
                dve.wait_ge(sem("scores_mm"), count(b, g, 2, h + 1))
                dve.tensor_reduce(bmax[:, head:head + 1], ps[:, SS:SS + 2, 0:HALF], mybir.AxisListType.XY, ALU.max)\
                    .then_inc(sem("block_max"), 1)
                dve.wait_ge(sem("block_max"), count(b, g, 2, h + 1))
                dve.tensor_scalar(nm_new[:, head:head + 1], bmax[:, head:head + 1], -1.0 / Q_UP, nm_old[:, head:head + 1],
                                  ALU.mult, ALU.min).then_inc(sem("nm_new"), 1)

            def p_low(b, g, h):
                for j, (t0, t1) in enumerate(TURNS):
                    dve.wait_ge(sem("p_hi"), count(b, g, 4, 2 * h + j + 1))
                    dve.scalar_tensor_tensor(out=prT[:, h, 1, t0 * P:t1 * P],
                                             in0=ps[:, TT + (2 * (h + 1) + j) % 3, 0:(t1 - t0) * P], scalar=P_UP,
                                             in1=prT[:, h, 0, t0 * P:t1 * P], op0=ALU.mult, op1=ALU.subtract)\
                        .then_inc(sem("p_lo"), 1)

            def carry(b, g, h):
                head = g * HPG + h
                dve.wait_ge(sem("pv_mm"), count(b, g, 2, h + 1))
                dve.wait_ge(sem("alpha"), count(b, g, 2, h + 1))
                dve.scalar_tensor_tensor(out=acc[:, head, :], in0=acc[:, head, :], scalar=alpha[:, head:head + 1],
                                         in1=ps[:, OO, 0:D], op0=ALU.mult, op1=ALU.add).then_inc(sem("o_done"), 1)
                dve.scalar_tensor_tensor(out=lsum[:, head:head + 1], in0=lsum[:, head:head + 1], scalar=alpha[:, head:head + 1],
                                         in1=rsum[:, head:head + 1], op0=ALU.mult, op1=ALU.add)
                dve.tensor_copy(nm_old[:, head:head + 1], nm_new[:, head:head + 1]).then_inc(sem("state"), 1)

            def step(b, g, last):
                project_on = not (last and g >= G - 2)
                b2, g2 = (b, g + 2) if g + 2 < G else (b + 1, g + 2 - G)
                row_max(b, g, 0)
                if project_on:
                    unit_out(b2, g2, 0)
                row_max(b, g, 1)
                if project_on:
                    unit_norm(b2, g2, 0)
                p_low(b, g, 0)
                if project_on:
                    unit_out(b2, g2, 1)
                carry(b, g, 0)
                if project_on:
                    unit_norm(b2, g2, 1)
                p_low(b, g, 1)
                if project_on:
                    unit_out(b2, g2, 2)
                    unit_norm(b2, g2, 2)
                carry(b, g, 1)
                if project_on:
                    unit_out(b2, g2, 3)
                    unit_norm(b2, g2, 3)

            for g in range(2):
                for u in range(len(UNITS)):
                    unit_out(0, g, u)
                    unit_norm(0, g, u)
            with dve.Fori(0, NBLK - 1) as b:
                for g in range(G):
                    step(b, g, False)
            for g in range(G):
                step(NBLK - 1, g, True)

            dve.wait_ge(sem("state"), NBLK * NH)
            link(dve.reciprocal(rden[:, :], lsum[:, :]))
            for h in range(NH):
                ins = dve.tensor_scalar(acc[:, h, :], acc[:, h, :], rden[:, h:h + 1], 1.0 / (V_UP * P_UP), ALU.mult, ALU.mult)
            ins.then_inc(sem("xout"), 1)
            for h in range(NH):
                dve.wait_ge(sem("xoutT_mm"), h // 4 + 1)
                k = 4 * NC + NH + h
                ins = dve.tensor_scalar(z_c[:, h, :], ps[:, h // 4, (h % 4) * T:(h % 4 + 1) * T], rcp_in[:, k:k + 1], FP8_MAX,
                                        ALU.mult, ALU.min)
            link(ins)
            link(dve.tensor_scalar(z_bf[:, :, :], z_c[:, :, :], -FP8_MAX, None, ALU.max))
            link(round_fp8(z_bf[:, :, :], z_f[:, :, :], z_c[:, :, :]))
            dve.tensor_copy(xoutq[:, :, :], z_f[:, :, :]).then_inc(sem("xoutq"), 1)
            link(dve.tensor_tensor(pscale[:, :], scalar("proj_in"), scalar("proj_w"), ALU.mult))
            dve.wait_ge(sem("proj_mm"), 1)
            link(dve.scalar_tensor_tensor(out=xs[:, :], in0=ps[:, 4, :], scalar=pscale[:, 0:1], in1=xs[:, :], op0=ALU.mult, op1=ALU.add))

            norm_row("a1", a_xn[:, :], xs[:, :])
            norm_row("a2", a_xn[:, :], a_xn[:, :], "a_xn")
            dve.wait_ge(sem("a_xT_mm"), 1)
            for c in range(NC):
                dve.tensor_scalar(a_xT[:, c, :], ps[:, 0, c * T:(c + 1) * T], col("ln_g2", c), col("ln_b2", c), ALU.mult, ALU.add)\
                    .then_inc(sem("a_xT"), 1)
            for k, (dst, mm, bias) in enumerate(((a_QT, "a_QT", "bq"), (a_KT, "a_KT", "bk"))):
                dve.wait_ge(sem(mm + "_mm"), 1)
                for m in range(NC):
                    dve.tensor_scalar(dst[:, m, :], ps[:, 1 + k, m * T:(m + 1) * T], col(bias, m), None, ALU.add)\
                        .then_inc(sem(mm), 1)
            dve.wait_ge(sem("a_V_mm"), 1)
            dve.tensor_tensor(a_V[:, :], ps[:, 3, :], rows[:, 0:C], ALU.add).then_inc(sem("a_V"), 1)
            dve.wait_ge(sem("causal"), 1)
            for j in range(4):
                dve.wait_ge(sem("a_scores_mm"), j + 1)
                for m in range(NC):
                    ins = dve.scalar_tensor_tensor(out=a_P[:, j, m, :], in0=ps[:, 4 + j, m * T:(m + 1) * T], scalar=SD ** -0.5,
                                                   in1=causal[:, :], op0=ALU.mult, op1=ALU.add)
            link(ins)
            link(dve.tensor_reduce(mx[:, :].rearrange("p (a b) -> p a b", a=4), a_P[:, :, :, :], AX, ALU.max))
            dve.tensor_scalar(nmx[:, :], mx[:, :], -1.0, None, ALU.mult).then_inc(sem("a_nmax"), 1)
            dve.wait_ge(sem("a_probs"), SH)
            link(dve.reciprocal(rden[:, :], den[:, :]))
            dve.wait_ge(sem("a_pv_mm"), 1)
            for k in range(SH):
                head = (k % 4) * 4 + k // 4
                ins = dve.tensor_scalar(a_o[:, head * SD:(head + 1) * SD], ps[:, 4, head * SD:(head + 1) * SD], rden[:, k:k + 1], None, ALU.mult)
            ins.then_inc(sem("a_o"), 1)
            dve.wait_ge(sem("a_oT_mm"), 1)
            dve.tensor_copy(a_oT[:, :, :], ps[:, 0, :].rearrange("p (c t) -> p c t", t=T)).then_inc(sem("a_oT"), 1)
            link(dve.tensor_tensor(xs[:, :], xs[:, :], rows[:, C:2 * C], ALU.add))
            dve.wait_ge(sem("a_out_mm"), 1)
            link(dve.tensor_tensor(xs[:, :], ps[:, 5, :], xs[:, :], ALU.add))

            norm_row("e1", a_xn[:, :], xs[:, :], "e_xn")
            dve.wait_ge(sem("e_xT_mm"), 1)
            dve.tensor_copy(a_xT[:, :, :], ps[:, 0, :].rearrange("p (c t) -> p c t", t=T)).then_inc(sem("e_xT"), 1)
            dve.wait_ge(sem("logits_mm"), 1)
            link(dve.tensor_reduce(mx[:, 0:1], ps[:, 1, 0:E], AX, ALU.max))
            dve.tensor_scalar(nmx[:, 0:1], mx[:, 0:1], -1.0, None, ALU.mult).then_inc(sem("e_nmax"), 1)
            dve.wait_ge(sem("e_exp"), 1)
            link(dve.reciprocal(rden[:, 0:1], den[:, 0:1]))
            link(dve.tensor_scalar(gate[:, :], gate[:, :], rden[:, 0:1], None, ALU.mult))
            link(dve.max(top8[:, :], gate[:, :]))
            link(dve.match_replace(gate2[:, :], top8[:, :], gate[:, :], -1.0))
            link(dve.tensor_reduce(den[:, 0:1], top8[:, :], AX, ALU.add))
            link(dve.reciprocal(rden[:, 0:1], den[:, 0:1]))
            link(dve.scalar_tensor_tensor(out=gate[:, :], in0=gate2[:, :], scalar=0.0, in1=gate[:, :], op0=ALU.is_lt, op1=ALU.mult))
            dve.tensor_scalar(gate[:, :], gate[:, :], rden[:, 0:1], None, ALU.mult).then_inc(sem("gate"), 1)
            dve.wait_ge(sem("gate"), 1)
            dve.memset(ysum[:, :], 0.0).then_inc(sem("ysum"), 1)
            with dve.Fori(0, E // SLOTS) as it:
                def turned(k):
                    dve.wait_ge(sem("hid_turn_mm"), it * SLOTS + (k + 1))
                    if k >= 2:
                        dve.wait_ge(sem("y_mm"), it * SLOTS + (k - 1))
                    dve.tensor_copy(hidT[:, k % 2, 0, :], ps[:, 4 + k % 2, 0:T]).then_inc(sem("hidT"), 1)
                    dve.tensor_copy(hidT[0:F - P, k % 2, 1, :], ps[0:F - P, 4 + k % 2, T:2 * T]).then_inc(sem("hidT"), 1)

                for k in range(SLOTS):
                    dve.wait_ge(sem("silu"), it * SLOTS + (k + 1))
                    if k >= 2:
                        dve.wait_ge(sem("hid_turn_mm"), it * SLOTS + (k - 1))
                    dve.scalar_tensor_tensor(out=hid[:, k % 2, :], in0=silu[:, k % 2, :],
                                             scalar=gate[:, bass.ds(it * SLOTS + k, 1)],
                                             in1=ps[:, 2 + k % 2, F:2 * F], op0=ALU.mult, op1=ALU.mult).then_inc(sem("hid"), 1)
                    if k:
                        turned(k - 1)
                turned(SLOTS - 1)
                dve.wait_ge(sem("y_mm"), it * SLOTS + SLOTS)
                dve.wait_ge(sem("ysum"), it + 1)
                dve.tensor_tensor(ysum[:, :], ps[:, 6, :], ysum[:, :], ALU.add).then_inc(sem("ysum"), 1)
            dve.wait_ge(sem("ysum"), E // SLOTS + 1)
            dve.tensor_tensor(xs[:, :], xs[:, :], ysum[:, :], ALU.add).then_inc(sem("final"), 1)


def kernel(**inputs):
    import numpy as np
    import concourse.bacc as bacc
    from concourse.bass_utils import run_bass_kernel_spmd

    a = {k: np.asarray(v) for k, v in inputs.items()}

    def columns(v):
        return v.reshape(-1, P).T

    xa = "L0_xattn_"
    parts = {"q_in": a[xa + "q_in_scale"], "qx_in": a[xa + "qx_in_scale"], "k_in": a[xa + "k_in_scale"],
             "v_in": a[xa + "v_in_scale"], "smooth": a[xa + "proj_smooth"], "ln_w": a[xa + "ln_w"], "ln_b": a[xa + "ln_b"],
             "ln_g2": a["L0_attn_ln_g"], "ln_b2": a["L0_attn_ln_b"], "bq": a["L0_attn_bq"], "bk": a["L0_attn_bk"]}
    for n in ("qln_w", "qln_b", "kln_w", "kln_b", "qxln_w", "qxln_b", "kxln_w", "kxln_b"):
        parts[n] = a[xa + n]
    cols = np.concatenate([columns(parts[n]) for n in COLS], axis=1)
    scalars = [a[xa + n].reshape(1) for n in ("wq_scale", "wqx_scale", "wk_scale", "wv_scale", "proj_w_scale", "proj_in_scale")]
    rows = np.concatenate([a["L0_attn_bv"], a["L0_attn_bo"], *scalars])
    wkv = a[xa + "w_kv_x"].reshape(2, G, D, C).transpose(3, 1, 0, 2).reshape(C, 2 * G * D)
    arrays = {
        "x": a["x"][0], "ctxT": a["ctx_2048"][0].T, "wqT": a[xa + "wq"].T, "wqxT": a[xa + "wqx"].T, "wkT": a[xa + "wk"].T,
        "wvT": a[xa + "wv"].T, "wkvT": wkv, "wprojT": a[xa + "wproj"].T, "cols": cols, "rows": rows,
        "Wq": a["L0_attn_Wq"], "Wk": a["L0_attn_Wk"], "Wv": a["L0_attn_Wv"], "Wo": a["L0_attn_Wo"], "wgT": a["L0_ffn_wg"].T,
        "w1v1": np.concatenate([a["L0_ffn_w1"], a["L0_ffn_v1"]], axis=2), "w2": a["L0_ffn_w2"],
    }
    arrays = {f"in_{k}": np.ascontiguousarray(v) for k, v in arrays.items()}
    nc = bacc.Bacc("TRN2", target_bir_lowering=False, num_devices=1)
    args = [nc.dram_tensor(k, v.shape, mybir.dt.from_np(v.dtype), kind="ExternalInput").ap() for k, v in arrays.items()]
    args.append(nc.dram_tensor("out_0", (T, C), F32, kind="ExternalOutput").ap())
    build(nc, *args)
    r = run_bass_kernel_spmd(nc, [arrays], core_ids=[0])
    return r.results[0]["out_0"].reshape(1, T, C)
```

```python
from contextlib import ExitStack

import concourse.bass as bass
from concourse import mybir

ALU = mybir.AluOpType
ACT = mybir.ActivationFunctionType
AX = mybir.AxisListType.X
F32 = mybir.dt.float32
F16 = mybir.dt.float16
BF16 = mybir.dt.bfloat16
I32 = mybir.dt.int32

P = 128
T = 128
C = 512
NC = C // P
D = 128
NH = 16
G = 8
HPG = NH // G
S_CTX = 12544
TILES = 7
BLK = TILES * P
NBLK = S_CTX // BLK
HALF = BLK // 2
EPS = 1e-5
FP8_MAX = 448.0
W_UP = 256.0
V_UP = 16.0
Q_UP = 16.0
P_UP = 4096.0
UNITS = [(0, 1), (2, 3), (4, 5), (6,)]
TURNS = [(0, 4), (4, 7)]
SH = 16
SD = C // SH
E = 32
K_TOP = 8
F = 192
SLOTS = 8
BIG = 1e30

COLS = {}
_at = 0
for _name, _n in (("q_in", NC), ("qx_in", NC), ("k_in", NC), ("v_in", NC), ("smooth", 2 * NH),
                  ("ln_w", NC), ("ln_b", NC), ("qln_w", 1), ("qln_b", 1), ("kln_w", 1), ("kln_b", 1),
                  ("qxln_w", 1), ("qxln_b", 1), ("kxln_w", 1), ("kxln_b", 1),
                  ("ln_g2", NC), ("ln_b2", NC), ("bq", NC), ("bk", NC)):
    COLS[_name] = (_at, _at + _n)
    _at += _n
N_COLS = _at
SCALARS = ("wq", "wqx", "wk", "wv", "proj_w", "proj_in")
ROWS = 2 * C + len(SCALARS)
LN_AT = {"qx": 0, "k": NH, "q": NH + G}
N_LN = 2 * NH + G
PROJ_ORDER = [*range(NH, NH + 10), *range(8), NH + 10, NH + 11, *range(8, NH), *range(NH + 12, 2 * NH)]
TURN_ORDER = (1, 2, 0, 3)
PIECES = (1, 2, 3, 0)


def build(nc, x, ctxT, wqT, wqxT, wkT, wvT, wkvT, wprojT, cols_in, rows_in, Wq, Wk, Wv, Wo, wgT, w1v1, w2, out):
    with ExitStack() as ctx:
        named = {}

        def sem(name):
            if name not in named:
                named[name] = ctx.enter_context(nc.semaphore(name))
            return named[name]

        base0 = nc.sbuf_base
        limit = nc.sbuf_usable_end
        size = {F32: 4, F16: 2, BF16: 2, I32: 4}

        class Place:
            def __init__(self, at):
                self.at = at

            def put(self, name, shape, dt):
                n = size[dt]
                for k in shape[1:]:
                    n *= k
                t = nc.alloc_sbuf_tensor_at(name, shape, dt, offset=self.at)
                self.at += (n + 31) // 32 * 32
                assert self.at <= limit, (name, self.at, limit)
                return t

        small = Place((base0 + 31) // 32 * 32)
        ident = small.put("ident", [P, P], F32)
        causal = small.put("causal", [P, P], F32)
        cols = small.put("cols", [P, N_COLS], F32)
        rcp_in = small.put("rcp_in", [P, 4 * NC + 2 * NH], F32)
        rows = small.put("rows", [P, ROWS], F32)
        neghalf = small.put("neghalf", [P, NH], F32)
        stat = small.put("stat", [P, NH, 6], F32)
        mv = small.put("mv", [P, NH, 2], F32)
        vare = small.put("vare", [P, NH], F32)
        rstd = small.put("rstd", [P, NH], F32)
        mx = small.put("mx", [P, NH], F32)
        nmx = small.put("nmx", [P, NH], F32)
        den = small.put("den", [P, NH], F32)
        rden = small.put("rden", [P, NH], F32)
        pscale = small.put("pscale", [P, 1], F32)
        kstat = small.put("kstat", [P, 2, 2, 6], F32)
        kmv = small.put("kmv", [P, 2, 2, 2], F32)
        kvar = small.put("kvar", [P, 2, 2], F32)
        krstd = small.put("krstd", [P, 2, 2], F32)
        bmax = small.put("bmax", [P, NH], F32)
        head_mul = small.put("head_mul", [P, N_LN], F32)
        head_add = small.put("head_add", [P, N_LN], F32)
        wscale2 = small.put("wscale2", [P, len(SCALARS)], F32)
        wscale_neg = small.put("wscale_neg", [P, len(SCALARS)], F32)
        qx_affine = small.put("qx_affine", [P, 2], F32)
        k_eps = small.put("k_eps", [P, 2], F32)
        nm_new = small.put("nm_new", [P, NH], F32)
        nm_old = small.put("nm_old", [P, NH], F32)
        alpha = small.put("alpha", [P, NH], F32)
        rsum = small.put("rsum", [P, NH], F32)
        lsum = small.put("lsum", [P, NH], F32)
        xs = small.put("xs", [P, C], F32)
        slot_x = Place(small.at)

        def expert_slot(place, k):
            return (place.put(f"w1v1_{k}", [P, NC, 2 * F], F32), place.put(f"w2a_{k}", [P, C], F32),
                    place.put(f"w2b_{k}", [P, C], F32))

        b0 = slot_x.at
        pb = Place(b0)
        wq_s = pb.put("wq_s", [P, NC, NH * D], F32)
        wk_s = pb.put("wk_s", [P, NC, G * D], F32)
        wv_s = pb.put("wv_s", [P, NC, G * D], F32)
        b1 = pb.at
        pb = Place(b0)
        qT = pb.put("qT", [P, NH, T], F32)
        probs = pb.put("probs", [P, NH, T], F32)
        probsT = pb.put("probsT", [P, NH, T], F32)
        pb = Place(b0 + NC * NH * D * 4)
        wkv_s = pb.put("wkv_s", [P, NC, 2 * G * D], F32)
        wproj_s = Place(b0).put("wproj_s", [P, 2 * NH, C], F32)
        pb = Place(b0)
        slots_b = [expert_slot(pb, k) for k in range(3, 9)]
        assert pb.at <= b1

        m0 = b1
        pm = Place(m0)
        coreq = pm.put("coreq", [P, NH, T], F32)
        w_hl = pm.put("w_hl", [P, 2, NC, G, 2 * D], F16)
        ctx_s = pm.put("ctx_s", [P, NC, BLK], F32)
        qx_hl = pm.put("qx_hl", [P, 2, NH, T], F16)
        m1 = pm.at
        ctx_hl = pm.put("ctx_hl", [P, 2, NC, BLK], F16)
        m_kn = pm.at
        kn = pm.put("kn", [P, 2, BLK], F32)
        khT = pm.put("khT", [P, 2, 2, BLK], F16)
        vhl = pm.put("vhl", [P, 4, 2, BLK], F16)
        kfull = pm.put("kfull", [P, BLK], F32)
        m_pr = pm.at
        pr = pm.put("pr", [P, 2, BLK], F32)
        prT = pm.put("prT", [P, 2, 2, BLK], F16)
        acc = pm.put("acc", [P, NH, D], F32)
        o_c = pm.put("o_c", [P, 4, T], F32)
        o_bf = pm.put("o_bf", [P, 4, T], BF16)
        z_c = pm.put("z_c", [P, HPG, T], F32)
        z_bf = pm.put("z_bf", [P, HPG, T], BF16)
        wqx_s = Place(m0 + NH * T * 4).put("wqx_s", [P, NC, NH * D], F32)
        pa = Place(m_kn)
        xn = pa.put("xn", [P, C], F32)
        lnT = pa.put("lnT", [P, NC, T], F32)
        y_bf = pa.put("y_bf", [P, 4 * NC, T], BF16)
        y_f = pa.put("y_f", [P, 4 * NC, T], F32)
        qx_sb = pa.put("qx_sb", [P, NH, D], F32)
        k_sb = pa.put("k_sb", [P, G, D], F32)
        assert pa.at <= m_pr
        qx_full = y_f
        pa = Place(m_pr)
        q_sb = pa.put("q_sb", [P, NH, D], F32)
        v_sb = pa.put("v_sb", [P, G * D], F32)
        khatT = pa.put("khatT", [P, G * D], F32)
        xq = pa.put("xq", [P, 4 * NC, T], F32)
        head_stat = pa.put("head_stat", [P, N_LN, 6], F32)
        head_mv = pa.put("head_mv", [P, N_LN, 2], F32)
        head_var = pa.put("head_var", [P, N_LN], F32)
        head_rstd = pa.put("head_rstd", [P, N_LN], F32)
        head_neg = pa.put("head_neg", [P, N_LN], F32)
        assert pa.at <= pm.at
        pd = Place(m0 + NH * T * 4)
        sw = [pd.put(f"sw{k}", [P, NC, C], F32) for k in range(4)]
        assert pd.at <= m0 + NH * T * 4 + 32768
        slots_a = [expert_slot(Place(m0 + NH * T * 4 + 32768), 0)]
        TAIL_AT = 2 * NC * BLK * 2 + 2 * BLK * 4 + 4 * BLK * 2 + 8 * BLK * 2
        pd = Place(m1 + TAIL_AT)
        a_xn = pd.put("a_xn", [P, C], F32)
        a_xT = pd.put("a_xT", [P, NC, T], F32)
        a_QT = pd.put("a_QT", [P, NC, T], F32)
        a_KT = pd.put("a_KT", [P, NC, T], F32)
        a_V = pd.put("a_V", [P, C], F32)
        a_o = pd.put("a_o", [P, C], F32)
        a_oT = pd.put("a_oT", [P, NC, T], F32)
        e_xhl = pd.put("e_xhl", [P, 2, NC, T], F16)
        wg_s = pd.put("wg_s", [P, NC, E], F32)
        gate = pd.put("gate", [P, E], F32)
        gate2 = pd.put("gate2", [P, E], F32)
        top8 = pd.put("top8", [P, K_TOP], F32)
        silu = pd.put("silu", [P, 2, F], F32)
        hid = pd.put("hid", [P, 2, F], F32)
        hidT = pd.put("hidT", [P, 2, 2, T], F32)
        zeros = pd.put("zeros", [P, P], F32)
        pd = Place(m1)
        a_P = pd.put("a_P", [P, 4, NC, T], F32)
        a_PT = pd.put("a_PT", [P, SH, T], F32)
        slots_c = [expert_slot(pd, 1)]
        up_hl = pd.put("up_hl", [P, 2, 2, NC, 2 * F], F16)
        assert pd.at <= m1 + TAIL_AT
        slots = (slots_a + slots_c + slots_b)[:SLOTS]
        SLOT_AFTER = ["context", "context", "proj", "proj", "proj", "proj", "proj", "proj"]

        ps = ctx.enter_context(nc.psum_tensor("ps", [P, 8, 512], F32))
        KV, TT, SS, OO = 0, 2, 5, 7

        def col(name, k=0):
            return cols[:, COLS[name][0] + k:COLS[name][0] + k + 1]

        def scalar(name):
            k = 2 * C + SCALARS.index(name)
            return rows[:, k:k + 1]

        def count(b, g, per_step, k):
            return b * (G * per_step) + (g * per_step + k)

        def on(b, g, k):
            return (b, g + k) if g + k < G else (b + 1, g + k - G)

        block = ctx.enter_context(nc.Block())

        @block.sync
        def _(sp):
            sp.dma_start(xs[:, :], x).then_inc(sem("x_in"), 16)
            sp.dma_start(cols[:, :], cols_in).then_inc(sem("cols_in"), 16)
            sp.dma_start(wqx_s[:, :, :], wqxT.rearrange("(c p) n -> p c n", p=P)).then_inc(sem("wqx_in"), 16)
            sp.dma_start(rows[:, :], rows_in.partition_broadcast(P)).then_inc(sem("rows_in"), 16)
            sp.dma_start(wk_s[:, :, :], wkT.rearrange("(c p) n -> p c n", p=P)).then_inc(sem("wk_in"), 16)
            sp.dma_start(wv_s[:, :, :], wvT.rearrange("(c p) n -> p c n", p=P)).then_inc(sem("wv_in"), 16)
            ctx_view = ctxT.rearrange("(c p) t -> p c t", p=P)
            sp.dma_start(ctx_s[:, :, :], ctx_view[:, :, 0:BLK]).then_inc(sem("ctx_in"), 16)
            sp.dma_start(wq_s[:, :, :], wqT.rearrange("(c p) n -> p c n", p=P)).then_inc(sem("wq_in"), 16)
            sp.wait_ge(sem("kproj_mm"), 2)
            sp.wait_ge(sem("vproj_mm"), 2)
            for half in range(2):
                n = slice(half * G * D, (half + 1) * G * D)
                sp.dma_start(wkv_s[:, :, n], wkvT.rearrange("(c p) n -> p c n", p=P)[:, :, n]).then_inc(sem(f"wkv_in{half}"), 16)
            sp.wait_ge(sem("coreT"), 4)
            sp.wait_ge(sem("wkv_lo"), G)
            sp.dma_start(wproj_s[:, :, :], wprojT.rearrange("(c p) n -> p c n", p=P)).then_inc(sem("wproj_in"), 16)
            with sp.Fori(0, NBLK - 1) as b:
                sp.wait_ge(sem("ctx_split"), b * TILES + TILES)
                sp.dma_start(ctx_s[:, :, :], ctx_view[:, :, bass.ds(b * BLK + BLK, BLK)]).then_inc(sem("ctx_in"), 16)

            def load_expert(slot, e):
                w13, wa, wb = slots[slot]
                s = sem(f"expert_in{slot}")
                sp.dma_start(w13[:, :, :], w1v1[e].rearrange("(c p) f -> p c f", p=P)).then_inc(s, 16)
                sp.dma_start(wa[:, :], w2[e][0:P, :]).then_inc(s, 16)
                sp.dma_start(wb[0:F - P, :], w2[e][P:F, :]).then_inc(s, 16)

            sp.wait_ge(sem("kv_mm"), NBLK * G * len(UNITS))
            for k, w in enumerate((Wq, Wk, Wv, Wo)):
                sp.dma_start(sw[k][:, :, :], w.rearrange("(c p) n -> p c n", p=P)).then_inc(sem(f"sw{k}_in"), 16)
            load_expert(0, 0)
            sp.wait_ge(sem("o_done"), NBLK * NH + 1)
            sp.dma_start(wg_s[:, :, :], wgT.rearrange("(c p) n -> p c n", p=P)).then_inc(sem("wg_in"), 16)
            sp.wait_ge(sem("proj_mm"), 1)
            for slot in range(1, SLOTS):
                load_expert(slot, slot)
            with sp.Fori(0, E // SLOTS - 1) as it:
                for slot in range(SLOTS):
                    sp.wait_ge(sem("y_mm"), it * SLOTS + (slot + 1))
                    w13, wa, wb = slots[slot]
                    e = it * SLOTS + (SLOTS + slot)
                    s = sem(f"expert_in{slot}")
                    sp.dma_start(w13[:, :, :], w1v1.rearrange("e (c p) f -> p (e c) f", p=P)[:, bass.ds(e * NC, NC), :]).then_inc(s, 16)
                    sp.dma_start(wa[:, :], w2[bass.ds(e, 1), 0:P, :].rearrange("o f n -> (o f) n")).then_inc(s, 16)
                    sp.dma_start(wb[0:F - P, :], w2[bass.ds(e, 1), P:F, :].rearrange("o f n -> (o f) n")).then_inc(s, 16)
            sp.wait_ge(sem("final"), 1)
            sp.dma_start(out, xs[:, :]).then_inc(sem("out_done"), 16)
            sp.wait_ge(sem("out_done"), 16)

        @block.tensor
        def _(pe):
            def transposes(dst_bank, src, n, signal, group=4):
                for k in range(n):
                    mm = pe.transpose(ps[:, dst_bank + k // group, (k % group) * P:(k % group + 1) * P], src(k), ident[:, :])
                    if k % group == group - 1 or k == n - 1:
                        mm.then_inc(sem(signal), 1)

            def project(bank, xT, w, n_blocks, signal):
                for n in range(n_blocks):
                    for c in range(NC):
                        mm = pe.matmul(ps[:, bank + n, :], xT[:, c, :], w[:, c, n * 512:(n + 1) * 512],
                                       start=(c == 0), stop=(c == NC - 1))
                    mm.then_inc(sem(signal), 1)

            def stay_warm(n, bank=7):
                for _ in range(n):
                    pe.transpose(ps[:, bank, 0:P], ident[:, :], ident[:, :])

            pe.wait_ge(sem("ident"), 1)
            stay_warm(16)
            pe.wait_ge(sem("xn"), 1)
            transposes(0, lambda k: xn[:, k * P:(k + 1) * P], NC, "xnT_mm")
            stay_warm(60)
            pe.wait_ge(sem("xq"), 1)
            pe.wait_ge(sem("wqx_in"), 16)
            project(4, xq[:, NC:2 * NC, :], wqx_s, 4, "qxproj_mm")
            pe.wait_ge(sem("xq"), 2)
            pe.wait_ge(sem("wk_in"), 16)
            project(0, xq[:, 2 * NC:3 * NC, :], wk_s, 2, "kproj_mm")
            pe.wait_ge(sem("qx_hat"), 4)
            transposes(4, lambda k: qx_sb[:, k, :], NH, "qxhatT_mm")
            pe.wait_ge(sem("xq"), 3)
            pe.wait_ge(sem("wv_in"), 16)
            project(2, xq[:, 3 * NC:4 * NC, :], wv_s, 2, "vproj_mm")
            pe.wait_ge(sem("k_hat"), 2)
            transposes(0, lambda k: k_sb[:, k, :], G, "khatT_mm")
            pe.wait_ge(sem("xq"), 4)
            pe.wait_ge(sem("wq_in"), 16)
            pe.wait_ge(sem("qxhatT"), 4)
            project(4, xq[:, 0:NC, :], wq_s, 4, "qproj_mm")

            def own_q_turn():
                for n in range(4):
                    pe.wait_ge(sem("q_hat"), n + 1)
                    for k in range(4 * n, 4 * n + 4):
                        mm = pe.transpose(ps[:, 4 + n, (k % 4) * D:(k % 4 + 1) * D], q_sb[:, k, :], ident[:, :])
                    mm.then_inc(sem("qhatT_mm"), 1)

            def own_scores():
                pe.wait_ge(sem("khatT"), 2)
                for h in range(NH):
                    if h % 4 == 0:
                        pe.wait_ge(sem("qhatT"), h // 4 + 1)
                    mm = pe.matmul(ps[:, 4 + h // 4, (h % 4) * T:(h % 4 + 1) * T], qT[:, h, :],
                                   khatT[:, (h // HPG) * P:(h // HPG + 1) * P], start=True, stop=True)
                mm.then_inc(sem("own_scores_mm"), 1)

            def own_p_turn():
                for n in range(4):
                    pe.wait_ge(sem("own_probs"), 4 * n + 4)
                    for k in range(4 * n, 4 * n + 4):
                        mm = pe.transpose(ps[:, 4 + n, (k % 4) * T:(k % 4 + 1) * T], probs[:, k, :], ident[:, :])
                    mm.then_inc(sem("own_probsT_mm"), 1)

            def own_outputs():
                for h in range(NH):
                    if h % 4 == 0:
                        pe.wait_ge(sem("own_probsT"), h // 4 + 1)
                    if h == 0:
                        pe.wait_ge(sem("v_sb"), 2)
                    mm = pe.matmul(ps[:, 4 + h // 4, (h % 4) * D:(h % 4 + 1) * D], probsT[:, h, :],
                                   v_sb[:, (h // HPG) * D:(h // HPG + 1) * D], start=True, stop=True)
                    if h % 4 == 3:
                        mm.then_inc(sem("own_pv_mm"), 1)

            def own_o_turn():
                for i, n in enumerate(TURN_ORDER):
                    pe.wait_ge(sem("core"), i + 1)
                    for k in range(4 * n, 4 * n + 4):
                        mm = pe.transpose(ps[:, 4 + n, (k % 4) * T:(k % 4 + 1) * T], q_sb[:, k, :], ident[:, :])
                    mm.then_inc(sem("coreT_mm"), 1)

            def kv_unit(b, g, u, in_block=None):
                if g == 0:
                    pe.wait_ge(sem("ctx_split"), b * TILES + (UNITS[u][-1] + 1))
                first = isinstance(b, int) and b == 0 and g == 0 and u < 2
                if not first:
                    pe.wait_ge(sem("k_norm"), count(b, g, 4, u - 1))
                for i, t in enumerate(UNITS[u]):
                    o = ps[:, KV + u % 2, i * 2 * D:(i + 1) * 2 * D]
                    for c in range(NC):
                        for xp, wp in ((0, 0), (0, 1), (1, 0)):
                            mm = pe.matmul(o, ctx_hl[:, xp, c, t * P:(t + 1) * P], w_hl[:, wp, c, g, :],
                                           start=(c == 0 and xp + wp == 0), stop=(c == NC - 1 and xp == 1))
                mm.then_inc(sem("kv_mm"), 1)

            def k_turn(b, g, ring_full=True, banks=(TT + 1, TT + 2)):
                pe.wait_ge(sem("k_norm"), count(b, g, 4, 4))
                for j, (t0, t1) in enumerate(TURNS):
                    if j == 1 and ring_full:
                        pe.wait_ge(sem("p_lo"), count(b, g - 2, 4, 3))
                    for t in range(t0, t1):
                        mm = pe.transpose(ps[:, banks[j], (t - t0) * P:(t - t0 + 1) * P], kn[:, g % 2, t * P:(t + 1) * P], ident[:, :])
                    mm.then_inc(sem("k_turn_mm"), 1)

            def scores(b, g, h):
                head = g * HPG + h
                if h == 0:
                    pe.wait_ge(sem("k_lo"), count(b, g, 2, 2))
                else:
                    pe.wait_ge(sem("probs"), count(b, g, 2, 1))
                for qp, kp in ((0, 0), (0, 1), (1, 0)):
                    for half in range(2):
                        mm = pe.matmul(ps[:, SS + half, 0:HALF], qx_hl[:, qp, head, :],
                                       khT[:, g % 2, kp, half * HALF:(half + 1) * HALF],
                                       start=(qp + kp == 0), stop=(qp == 1), skip_group_check=True)
                mm.then_inc(sem("scores_mm"), 1)

            def p_turn(b, g, h, keys_turned):
                pe.wait_ge(sem("probs"), count(b, g, 2, h + 1))
                for j, (t0, t1) in enumerate(TURNS):
                    bank = TT + (2 * h + j) % 3
                    if keys_turned and h != j:
                        pe.wait_ge(sem("k_full"), count(b, g + 1, 2, h + 1))
                    if (h, j) == (1, 1):
                        pe.wait_ge(sem("p_lo"), count(b, g, 4, 1))
                    for t in range(t0, t1):
                        mm = pe.transpose(ps[:, bank, (t - t0) * P:(t - t0 + 1) * P], pr[:, h, t * P:(t + 1) * P], ident[:, :])
                    mm.then_inc(sem("p_turn_mm"), 1)

            def outputs(b, g, h):
                pe.wait_ge(sem("p_lo"), count(b, g, 4, 2 * h + 2))
                if h == 0:
                    pe.wait_ge(sem("v_lo"), count(b, g, 4, 4))
                pe.wait_ge(sem("o_done"), count(b, g, 2, h + 1))
                for t in range(TILES):
                    tile = slice(t * P, (t + 1) * P)
                    pe.matmul(ps[:, OO, 0:2 * D].rearrange("p (a d) -> p a d", a=2), prT[:, h, 0, tile], vhl[:, g % 4, :, tile],
                              start=(t == 0), stop=False)
                    mm = pe.matmul(ps[:, OO, 0:D], prT[:, h, 1, tile], vhl[:, g % 4, 0, tile], start=False, stop=(t == TILES - 1))
                mm.then_inc(sem("pv_mm"), 1)

            def x_turn(g):
                pe.wait_ge(sem("xout"), g + 1)
                if g < G - 1:
                    pe.wait_ge(sem("p_lo"), count(NBLK - 1, g + 1, 4, 2))
                for h in range(HPG):
                    mm = pe.transpose(ps[:, TT + 1, h * T:(h + 1) * T], acc[:, g * HPG + h, :], ident[:, :])
                mm.then_inc(sem("x_turn_mm"), 1)

            projected = [0]

            def out_project(n):
                for i in range(projected[0], min(projected[0] + n, 2 * NH)):
                    k = PROJ_ORDER[i]
                    if i == 0:
                        pe.wait_ge(sem("k_norm"), NBLK * G * len(UNITS) - 1)
                        pe.wait_ge(sem("wproj_in"), 16)
                    if k < NH and k % 4 == 0:
                        pe.wait_ge(sem("coreq"), k // 4 + 1)
                    if k >= NH and k % HPG == 0:
                        pe.wait_ge(sem("xoutq"), (k - NH) // HPG + 1)
                    mm = pe.matmul(ps[:, KV, :], coreq[:, k, :] if k < NH else acc[:, k - NH, :], wproj_s[:, k, :],
                                   start=(i == 0), stop=(i == 2 * NH - 1))
                    projected[0] = i + 1
                if projected[0] == 2 * NH and n:
                    mm.then_inc(sem("proj_mm"), 1)

            def step(b, g, last):
                ahead = G - g if last else NBLK * G
                scores(b, g, 1)
                if last and g == G - 1:
                    pe.wait_ge(sem("x_taken"), G - 2)
                p_turn(b, g, 0, ahead > 1)
                if ahead > 2:
                    kv_unit(*on(b, g, 2), 1)
                    kv_unit(*on(b, g, 2), 2)
                if last and ahead <= 2:
                    out_project(3)
                if last and g:
                    x_turn(g - 1)
                if last and ahead <= 2:
                    out_project(3)
                p_turn(b, g, 1, ahead > 1)
                outputs(b, g, 0)
                if ahead > 2:
                    kv_unit(*on(b, g, 2), 3)
                if ahead > 1:
                    scores(*on(b, g, 1), 0)
                if last and ahead <= 3:
                    out_project(4 if ahead == 3 else 7)
                if ahead > 3:
                    kv_unit(*on(b, g, 3), 0)
                if ahead > 2:
                    if last and g:
                        pe.wait_ge(sem("x_taken"), g)
                    k_turn(b, g + 2)
                outputs(b, g, 1)

            pe.wait_ge(sem("khatT"), 2)
            pe.wait_ge(sem("wkv_lo"), 1)
            kv_unit(0, 0, 0)
            kv_unit(0, 0, 1)
            own_q_turn()
            kv_unit(0, 0, 2)
            own_scores()
            kv_unit(0, 0, 3)
            pe.wait_ge(sem("wkv_lo"), 2)
            kv_unit(0, 1, 0)
            pe.wait_ge(sem("v_sb"), 2)
            k_turn(0, 0, ring_full=False, banks=(TT + 1, TT))
            own_p_turn()
            kv_unit(0, 1, 1)
            own_outputs()
            kv_unit(0, 1, 2)
            own_o_turn()
            kv_unit(0, 1, 3)
            pe.wait_ge(sem("qx_lo"), 4)
            pe.wait_ge(sem("coreT"), 2)
            scores(0, 0, 0)
            pe.wait_ge(sem("wkv_lo"), 3)
            kv_unit(0, 2, 0)
            pe.wait_ge(sem("k_full"), 2)
            pe.wait_ge(sem("coreT"), 4)
            k_turn(0, 1, ring_full=False)
            pe.wait_ge(sem("wkv_lo"), G)
            with pe.Fori(0, NBLK - 1) as b:
                for g in range(G):
                    step(b, g, False)
            for g in range(G):
                step(NBLK - 1, g, True)

            out_project(2 * NH - HPG - projected[0])
            pe.wait_ge(sem("x_taken"), G - 1)
            x_turn(G - 1)
            stay_warm(24, SS)
            out_project(HPG)
            stay_warm(24, SS)

            pe.wait_ge(sem("a_xn"), 1)
            transposes(0, lambda k: a_xn[:, k * P:(k + 1) * P], NC, "a_xT_mm")
            pe.wait_ge(sem("a_xT"), NC)
            for k, (w, signal) in enumerate(((0, "a_QT_mm"), (1, "a_KT_mm"))):
                pe.wait_ge(sem(f"sw{w}_in"), 16)
                for m in range(NC):
                    for c in range(NC):
                        mm = pe.matmul(ps[:, 1 + k, m * T:(m + 1) * T], sw[w][:, c, m * P:(m + 1) * P], a_xT[:, c, :],
                                       start=(c == 0), stop=(c == NC - 1))
                mm.then_inc(sem(signal), 1)
            pe.wait_ge(sem("sw2_in"), 16)
            project(3, a_xT, sw[2], 1, "a_V_mm")
            pe.wait_ge(sem("a_QT"), NC)
            pe.wait_ge(sem("a_KT"), NC)
            for j in range(4):
                for m in range(NC):
                    mm = pe.matmul(ps[:, 4 + j, m * T:(m + 1) * T], a_QT[j * SD:(j + 1) * SD, m, :],
                                   a_KT[j * SD:(j + 1) * SD, m, :], start=True, stop=True)
                mm.then_inc(sem("a_scores_mm"), 1)
            for j in range(4):
                pe.wait_ge(sem("a_probs"), 4 * j + 4)
                if j == 3:
                    pe.wait_ge(sem("a_V"), 1)
                for m in range(NC):
                    mm = pe.transpose(ps[:, j, m * T:(m + 1) * T], a_P[:, j, m, :], ident[:, :])
                mm.then_inc(sem("a_PT_mm"), 1)
            pe.wait_ge(sem("a_PT"), 4)
            for k in range(SH):
                head = (k % 4) * 4 + k // 4
                mm = pe.matmul(ps[:, 4, head * SD:(head + 1) * SD], a_PT[:, k, :], a_V[:, head * SD:(head + 1) * SD],
                               start=True, stop=True)
            mm.then_inc(sem("a_pv_mm"), 1)
            stay_warm(20)
            pe.wait_ge(sem("a_o"), 1)
            transposes(0, lambda k: a_o[:, k * P:(k + 1) * P], NC, "a_oT_mm")
            stay_warm(8)
            pe.wait_ge(sem("a_oT"), 1)
            pe.wait_ge(sem("sw3_in"), 16)
            project(5, a_oT, sw[3], 1, "a_out_mm")
            stay_warm(24)

            pe.wait_ge(sem("e_xn"), 1)
            transposes(0, lambda k: a_xn[:, k * P:(k + 1) * P], NC, "e_xT_mm")
            stay_warm(8)
            pe.wait_ge(sem("e_xT"), 1)
            pe.wait_ge(sem("wg_in"), 16)
            for c in range(NC):
                mm = pe.matmul(ps[:, 1, 0:E], a_xT[:, c, :], wg_s[:, c, :], start=(c == 0), stop=(c == NC - 1))
            mm.then_inc(sem("logits_mm"), 1)
            pe.wait_ge(sem("e_xT"), 2)

            def up(it, k):
                pe.wait_ge(sem("up_lo"), it * SLOTS + (k + 1))
                if k >= 2:
                    pe.wait_ge(sem("hid"), it * SLOTS + (k - 1))
                for c in range(NC):
                    for xp, wp in ((0, 0), (0, 1), (1, 0)):
                        mm = pe.matmul(ps[:, 2 + k % 2, 0:2 * F], e_xhl[:, xp, c, :], up_hl[:, k % 2, wp, c, :],
                                       start=(c == 0 and xp + wp == 0), stop=(c == NC - 1 and xp == 1))
                mm.then_inc(sem("up_mm"), 1)

            def experts(it, last):
                def turn(k):
                    pe.wait_ge(sem("hid"), it * SLOTS + (k + 1))
                    if k >= 2:
                        pe.wait_ge(sem("hidT"), it * (2 * SLOTS) + (2 * k - 2))
                    pe.transpose(ps[:, 4 + k % 2, 0:T], hid[:, k % 2, 0:P], ident[:, :])
                    pe.transpose(ps[0:F - P, 4 + k % 2, T:2 * T], hid[:, k % 2, P:F], ident[:, :]).then_inc(sem("hid_turn_mm"), 1)

                def down(k):
                    pe.wait_ge(sem("hidT"), it * (2 * SLOTS) + (2 * k + 2))
                    pe.matmul(ps[:, 6, :], hidT[:, k % 2, 0, :], slots[k][1][:, :], start=False, stop=False)
                    pe.matmul(ps[:, 6, :], hidT[0:F - P, k % 2, 1, :], slots[k][2][0:F - P, :], start=False,
                              stop=(last and k == SLOTS - 1)).then_inc(sem("y_mm"), 1)

                for k in range(SLOTS):
                    if not last or k + 1 < SLOTS:
                        up(it, k + 1)
                    turn(k)
                    if k:
                        down(k - 1)
                down(SLOTS - 1)

            pe.wait_ge(sem("zeros"), 1)
            pe.matmul(ps[:, 6, :], zeros[:, :], xs[:, :], start=True, stop=False)
            up(0, 0)
            with pe.Fori(0, E // SLOTS - 1) as it:
                experts(it, False)
            experts(E // SLOTS - 1, True)

        @block.scalar
        def _(act):
            def ctx_high(b, t):
                if t == 0:
                    act.wait_ge(sem("ctx_in"), b * 16 + 16)
                sl = slice(t * P, (t + 1) * P)
                act.activation(ctx_hl[:, 0, :, sl], ctx_s[:, :, sl], ACT.Copy).then_inc(sem("ctx_high"), 1)

            for n, piece in enumerate(PIECES):
                act.wait_ge(sem("y_f"), n + 1)
                for k in range(piece * NC, (piece + 1) * NC):
                    ins = act.activation(xq[:, k, :], y_f[:, k, :], ACT.Copy, scale=cols[:, k:k + 1])
                ins.then_inc(sem("xq"), 1)

            def normalise(tag, n, dst, bank):
                act.wait_ge(sem(f"own_{tag}_mul"), n + 1)
                for h in range(4):
                    k = LN_AT[tag] + 4 * n + h
                    ins = act.activation(dst[:, 4 * n + h, :], ps[:, bank + n, h * D:(h + 1) * D], ACT.Identity,
                                         bias=head_add[:, k:k + 1], scale=head_mul[:, k:k + 1])
                ins.then_inc(sem(f"{tag}_hat"), 1)

            for n in range(4):
                normalise("qx", n, qx_sb, 4)
            for n in range(2):
                normalise("k", n, k_sb, 0)
            act.wait_ge(sem("qx_affine"), 1)
            for n in range(4):
                act.wait_ge(sem("qxhatT_mm"), n + 1)
                src = ps[:, 4 + n, :].rearrange("p (a d) -> p a d", d=D)
                act.activation(qx_hl[:, 0, 4 * n:4 * n + 4, :], src, ACT.Identity, bias=qx_affine[:, 1:2], scale=qx_affine[:, 0:1])
                act.activation(qx_full[:, 4 * n:4 * n + 4, :], src, ACT.Identity, bias=qx_affine[:, 1:2], scale=qx_affine[:, 0:1])\
                   .then_inc(sem("qxhatT"), 1)
            for t in range(TILES):
                ctx_high(0, t)
            for n in range(2):
                act.wait_ge(sem("vproj_mm"), n + 1)
                act.activation(v_sb[:, n * 512:(n + 1) * 512], ps[:, 2 + n, :], ACT.Copy, scale=scalar("wv")).then_inc(sem("v_sb"), 1)
            for n in range(2):
                act.wait_ge(sem("khatT_mm"), n + 1)
                act.activation(khatT[:, n * 512:(n + 1) * 512], ps[:, n, :], ACT.Identity, bias=col("kln_b"),
                               scale=col("kln_w")).then_inc(sem("khatT"), 1)

            def wkv_high(g):
                if g % (G // 2) == 0:
                    act.wait_ge(sem(f"wkv_in{g // (G // 2)}"), 16)
                act.activation(w_hl[:, 0, :, g, :], wkv_s[:, :, g * 2 * D:(g + 1) * 2 * D], ACT.Copy, scale=W_UP)\
                   .then_inc(sem("wkv_hi"), 1)

            for n in range(4):
                wkv_high(n)
            for n in range(4):
                normalise("q", n, q_sb, 4)
                if n == 0:
                    wkv_high(4)

            def own_turned(dst, n, signal, **affine):
                act.wait_ge(sem(f"{signal}_mm"), n + 1)
                act.activation(dst[:, 4 * n:4 * n + 4, :], ps[:, 4 + n, :].rearrange("p (a d) -> p a d", d=D),
                               ACT.Identity if affine else ACT.Copy, **affine).then_inc(sem(signal), 1)

            def v_high(b, g, u):
                act.wait_ge(sem("kv_mm"), count(b, g, 4, u + 1))
                n, t0 = len(UNITS[u]), UNITS[u][0]
                act.activation(vhl[:, g % 4, 0, t0 * P:(t0 + n) * P].rearrange("p (t d) -> p t d", d=D),
                               ps[:, KV + u % 2, 0:n * 2 * D].rearrange("p (t k d) -> p t k d", k=2, d=D)[:, :, 1, :], ACT.Copy,
                               scale=V_UP / W_UP).then_inc(sem("v_hi"), 1)

            def k_affine(b, g, first=False, banks=(TT + 1, TT + 2)):
                for j, (t0, t1) in enumerate(TURNS):
                    src = ps[:, banks[j], 0:(t1 - t0) * P]
                    act.wait_ge(sem("k_turn_mm"), count(b, g, 2, j + 1))
                    act.activation(khT[:, g % 2, 0, t0 * P:t1 * P], src, ACT.Identity, bias=col("kxln_b"),
                                   scale=col("kxln_w")).then_inc(sem("k_hi"), 1)
                    if not first:
                        act.wait_ge(sem("k_lo"), count(b, g, 2, j - 1))
                    act.activation(kfull[:, t0 * P:t1 * P], src, ACT.Identity, bias=col("kxln_b"),
                                   scale=col("kxln_w")).then_inc(sem("k_full"), 1)

            def exps(b, g, h):
                head = g * HPG + h
                act.wait_ge(sem("nm_new"), count(b, g, 2, h + 1))
                act.activation(pr[:, h, :].rearrange("p (a n) -> p a n", a=2), ps[:, SS:SS + 2, 0:HALF], ACT.Exp,
                               bias=nm_new[:, head:head + 1], scale=1.0 / Q_UP,
                               accum_out=rsum[:, head:head + 1]).then_inc(sem("probs"), 1)
                act.activation(alpha[:, head:head + 1], nm_old[:, head:head + 1], ACT.Exp, bias=nm_new[:, head:head + 1],
                               scale=-1.0).then_inc(sem("alpha"), 1)

            def p_high(b, g, h):
                for j, (t0, t1) in enumerate(TURNS):
                    act.wait_ge(sem("p_turn_mm"), count(b, g, 4, 2 * h + j + 1))
                    act.activation(prT[:, h, 0, t0 * P:t1 * P], ps[:, TT + (2 * h + j) % 3, 0:(t1 - t0) * P], ACT.Copy,
                                   scale=P_UP).then_inc(sem("p_hi"), 1)

            def step(b, g, last):
                ahead = G - g if last else NBLK * G
                split_on = g == G - 3 and not last

                def split(u):
                    if split_on:
                        act.wait_ge(sem("kv_mm"), count(b, G - 1, 4, u + 1))
                        for t in UNITS[u]:
                            ctx_high(b + 1, t)

                split(0)
                p_high(b, g, 0)
                exps(b, g, 1)
                if ahead > 2:
                    v_high(*on(b, g, 2), 1)
                    split(1)
                    v_high(*on(b, g, 2), 2)
                p_high(b, g, 1)
                split(2)
                if ahead > 2:
                    v_high(*on(b, g, 2), 3)
                split(3)
                if ahead > 1:
                    exps(*on(b, g, 1), 0)
                if ahead > 3:
                    v_high(*on(b, g, 3), 0)
                if ahead > 2:
                    k_affine(*on(b, g, 2))

            v_high(0, 0, 0)
            wkv_high(5)
            v_high(0, 0, 1)
            for n in range(4):
                own_turned(qT, n, "qhatT", bias=col("qln_b"), scale=col("qln_w"))
            wkv_high(6)
            v_high(0, 0, 2)
            v_high(0, 0, 3)
            wkv_high(7)
            act.wait_ge(sem("own_nmax"), 1)
            for h in range(NH):
                act.activation(probs[:, h, :], ps[:, 4 + h // 4, (h % 4) * T:(h % 4 + 1) * T], ACT.Exp, bias=nmx[:, h:h + 1],
                               scale=D ** -0.5, accum_out=den[:, h:h + 1]).then_inc(sem("own_probs"), 1)
            v_high(0, 1, 0)
            k_affine(0, 0, first=True, banks=(TT + 1, TT))
            for n in range(4):
                own_turned(probsT, n, "own_probsT")
            v_high(0, 1, 1)
            act.wait_ge(sem("own_rden"), 1)
            act.wait_ge(sem("own_pv_mm"), 4)
            for n in TURN_ORDER:
                for h in range(4 * n, 4 * n + 4):
                    ins = act.activation(q_sb[:, h, :], ps[:, 4 + n, (h % 4) * D:(h % 4 + 1) * D], ACT.Copy, scale=rden[:, h:h + 1])
                ins.then_inc(sem("core"), 1)
            v_high(0, 1, 2)
            for i, n in enumerate(TURN_ORDER):
                act.wait_ge(sem("coreT_mm"), i + 1)
                for h in range(4 * n, 4 * n + 4):
                    ins = act.activation(coreq[:, h, :], ps[:, 4 + n, (h % 4) * T:(h % 4 + 1) * T], ACT.Copy,
                                         scale=rcp_in[:, 4 * NC + h:4 * NC + h + 1])
                ins.then_inc(sem("coreT"), 1)
            v_high(0, 1, 3)
            exps(0, 0, 0)
            v_high(0, 2, 0)
            k_affine(0, 1)
            with act.Fori(0, NBLK - 1) as b:
                for g in range(G):
                    step(b, g, False)
            for g in range(G):
                step(NBLK - 1, g, True)

            def up_high(it, k):
                it, k = (it, k) if k < SLOTS else (it + 1, k - SLOTS)
                act.wait_ge(sem(f"expert_in{k}"), it * 48 + 48)
                act.activation(up_hl[:, k % 2, 0, :, :], slots[k][0][:, :, :], ACT.Copy, scale=W_UP).then_inc(sem("up_hi"), 1)

            act.wait_ge(sem("proj_mm"), 1)
            up_high(0, 0)
            up_high(0, 1)

            for k in range(SH):
                act.wait_ge(sem("a_nmax"), k // 4 + 1)
                act.activation(a_P[:, k // 4, k % 4, :], a_P[:, k // 4, k % 4, :], ACT.Exp, bias=nmx[:, k:k + 1],
                               accum_out=den[:, k:k + 1]).then_inc(sem("a_probs"), 1)
            for n in range(4):
                act.wait_ge(sem("a_PT_mm"), n + 1)
                act.activation(a_PT[:, 4 * n:4 * n + 4, :], ps[:, n, :].rearrange("p (a d) -> p a d", d=T), ACT.Copy)\
                   .then_inc(sem("a_PT"), 1)
            act.wait_ge(sem("e_nmax"), 1)
            act.activation(gate[:, :], ps[:, 1, 0:E], ACT.Exp, bias=nmx[:, 0:1], accum_out=den[:, 0:1]).then_inc(sem("e_exp"), 1)
            def experts(it, last):
                for k in range(SLOTS):
                    act.wait_ge(sem("up_mm"), it * SLOTS + (k + 1))
                    if k >= 2:
                        act.wait_ge(sem("hid"), it * SLOTS + (k - 1))
                    act.activation(silu[:, k % 2, :], ps[:, 2 + k % 2, 0:F], ACT.Silu, scale=1.0 / W_UP).then_inc(sem("silu"), 1)
                    if not last or k + 2 < SLOTS:
                        up_high(it, k + 2)

            with act.Fori(0, E // SLOTS - 1) as it:
                experts(it, False)
            experts(E // SLOTS - 1, True)

        @block.gpsimd
        def _(pool):
            links = [0]

            def link(ins):
                links[0] += 1
                ins.then_inc(sem("pool_link"), 1)
                pool.wait_ge(sem("pool_link"), links[0])

            link(pool.memset(ident[:, :], 0.0))
            pool.affine_select(out=ident[:, :], in_=ident[:, :], compare_op=ALU.not_equal, fill=1.0, base=0,
                               pattern=[[-1, P]], channel_multiplier=1).then_inc(sem("ident"), 1)
            link(pool.memset(causal[:, :], 0.0))
            pool.affine_select(out=causal[:, :], in_=causal[:, :], compare_op=ALU.is_ge, fill=-BIG, base=0,
                               pattern=[[-1, P]], channel_multiplier=1).then_inc(sem("causal"), 1)
            link(pool.memset(neghalf[:, :], -0.5))
            link(pool.memset(k_eps[:, :], EPS * W_UP * W_UP))

            def rstd_row(tag, twice):
                pool.wait_ge(sem(f"var_{tag}"), 1)
                mul, add = (1.0 + EPS, EPS * EPS) if twice else (1.0, EPS)
                link(pool.tensor_scalar(vare[:, 0:1], mv[:, 0:1, 1], mul, add, ALU.mult, ALU.add))
                pool.tensor_tensor(rstd[:, 0:1], vare[:, 0:1], neghalf[:, 0:1], ALU.pow).then_inc(sem(f"rstd_{tag}"), 1)

            rstd_row("x", True)
            pool.wait_ge(sem("rows_in"), 16)
            link(pool.tensor_tensor(wscale2[:, :], rows[:, 2 * C:ROWS], rows[:, 2 * C:ROWS], ALU.mult))
            link(pool.tensor_scalar(wscale_neg[:, :], rows[:, 2 * C:ROWS], -1.0, None, ALU.mult))

            def normaliser(tag, n):
                at = LN_AT[tag] + 4 * n
                k = SCALARS.index("w" + tag)
                sl = slice(at, at + 4)
                pool.wait_ge(sem(f"own_{tag}_var"), n + 1)
                link(pool.tensor_scalar(head_var[:, sl], head_mv[:, sl, 1], wscale2[:, k:k + 1], EPS, ALU.mult, ALU.add))
                link(pool.tensor_tensor(head_rstd[:, sl], head_var[:, sl], neghalf[:, 0:4], ALU.pow))
                pool.tensor_scalar(head_mul[:, sl], head_rstd[:, sl], rows[:, 2 * C + k:2 * C + k + 1], None, ALU.mult)
                link(pool.tensor_scalar(head_neg[:, sl], head_rstd[:, sl], wscale_neg[:, k:k + 1], None, ALU.mult))
                pool.tensor_tensor(head_add[:, sl], head_mv[:, sl, 0], head_neg[:, sl], ALU.mult).then_inc(sem(f"own_{tag}_mul"), 1)

            def split_tile(b, t):
                sl = slice(t * P, (t + 1) * P)
                pool.wait_ge(sem("ctx_high"), b * TILES + (t + 1))
                pool.tensor_tensor(ctx_hl[:, 1, :, sl], ctx_s[:, :, sl], ctx_hl[:, 0, :, sl], ALU.subtract)\
                    .then_inc(sem("ctx_split"), 1)

            for n in range(4):
                normaliser("qx", n)
            for n in range(2):
                normaliser("k", n)
            for t in range(TILES):
                split_tile(0, t)
            for n in range(4):
                normaliser("q", n)

            def k_rstd(b, g, u):
                n = len(UNITS[u])
                pool.wait_ge(sem("k_var"), count(b, g, 4, u + 1))
                pool.tensor_tensor(kvar[:, u % 2, 0:n], kmv[:, u % 2, 0:n, 1], k_eps[:, 0:n], ALU.add)\
                    .then_inc(sem("k_vare"), 1)
                pool.wait_ge(sem("k_vare"), count(b, g, 4, u + 1))
                pool.tensor_tensor(krstd[:, u % 2, 0:n], kvar[:, u % 2, 0:n], neghalf[:, 0:n], ALU.pow).then_inc(sem("k_rstd"), 1)

            def k_low(b, g):
                for j, (t0, t1) in enumerate(TURNS):
                    sl = slice(t0 * P, t1 * P)
                    pool.wait_ge(sem("k_full"), count(b, g, 2, j + 1))
                    pool.tensor_tensor(khT[:, g % 2, 1, sl], kfull[:, sl], khT[:, g % 2, 0, sl], ALU.subtract)\
                        .then_inc(sem("k_lo"), 1)

            def step(b, g, last):
                ahead = G - g if last else NBLK * G

                def split(u):
                    if g == G - 3 and not last:
                        for t in UNITS[u]:
                            split_tile(b + 1, t)

                split(0)
                if ahead > 2:
                    for u in range(1, len(UNITS)):
                        k_rstd(*on(b, g, 2), u)
                        split(u)
                if ahead > 3:
                    k_rstd(*on(b, g, 3), 0)
                if ahead > 2:
                    k_low(*on(b, g, 2))

            for u in range(len(UNITS)):
                k_rstd(0, 0, u)
            pool.wait_ge(sem("own_scores_mm"), 1)
            pool.memset(acc[:, :, :], 0.0).then_inc(sem("o_done"), 1)
            k_low(0, 0)
            for u in range(len(UNITS)):
                k_rstd(0, 1, u)
            k_rstd(0, 2, 0)
            k_low(0, 1)
            with pool.Fori(0, NBLK - 1) as b:
                for g in range(G):
                    step(b, g, False)
            for g in range(G):
                step(NBLK - 1, g, True)
            rstd_row("a", True)
            rstd_row("e", False)

        @block.vector
        def _(dve):
            links = [0]

            def link(ins):
                links[0] += 1
                ins.then_inc(sem("dve_link"), 1)
                dve.wait_ge(sem("dve_link"), links[0])

            def norm_row(tag, dst, src, signal):
                link(dve.bn_stats(stat[:, 0, :], src))
                dve.bn_aggr(mv[:, 0, :], stat[:, 0, :]).then_inc(sem(f"var_{tag}"), 1)
                dve.wait_ge(sem(f"var_{tag}"), 1)
                dve.wait_ge(sem(f"rstd_{tag}"), 1)
                dve.tensor_scalar(dst, src, mv[:, 0, 0:1], rstd[:, 0:1], ALU.subtract, ALU.mult).then_inc(sem(signal), 1)

            def head_stats(tag, n, bank):
                dve.wait_ge(sem(f"{tag}proj_mm"), n + 1)
                for h in range(4):
                    ins = dve.bn_stats(head_stat[:, LN_AT[tag] + 4 * n + h, :], ps[:, bank + n, h * D:(h + 1) * D])
                link(ins)
                for h in range(4):
                    ins = dve.bn_aggr(head_mv[:, LN_AT[tag] + 4 * n + h, :], head_stat[:, LN_AT[tag] + 4 * n + h, :])
                ins.then_inc(sem(f"own_{tag}_var"), 1)

            def round_fp8(y_bf_, y_f_, y_c_):
                link(dve.tensor_copy(y_f_, y_bf_))
                link(dve.tensor_scalar(y_c_.bitcast(I32), y_f_.bitcast(I32), 0x7F800000, None, ALU.bitwise_and))
                link(dve.tensor_scalar(y_c_, y_c_, 2.0 ** -6, 1.5 * 2.0 ** 20, ALU.max, ALU.mult))
                link(dve.tensor_tensor(y_f_, y_f_, y_c_, ALU.add))
                return dve.tensor_tensor(y_f_, y_f_, y_c_, ALU.subtract)

            dve.wait_ge(sem("x_in"), 16)
            norm_row("x", xn[:, :], xs[:, :], "xn")
            dve.wait_ge(sem("cols_in"), 16)
            link(dve.reciprocal(rcp_in[:, :], cols[:, 0:4 * NC + 2 * NH]))
            dve.wait_ge(sem("xnT_mm"), 1)
            for c in range(NC):
                ins = dve.tensor_scalar(lnT[:, c, :], ps[:, 0, c * T:(c + 1) * T], col("ln_w", c), col("ln_b", c), ALU.mult, ALU.add)
            link(ins)
            for piece in PIECES:
                k0 = piece * NC
                part = slice(k0, k0 + NC)
                for k in range(k0, k0 + NC):
                    ins = dve.tensor_scalar(xq[:, k, :], lnT[:, k - k0, :], rcp_in[:, k:k + 1], FP8_MAX, ALU.mult, ALU.min)
                link(ins)
                link(dve.tensor_scalar(y_bf[:, part, :], xq[:, part, :], -FP8_MAX, None, ALU.max))
                round_fp8(y_bf[:, part, :], y_f[:, part, :], xq[:, part, :]).then_inc(sem("y_f"), 1)
            dve.tensor_scalar(qx_affine[:, :], cols[:, COLS["qxln_w"][0]:COLS["qxln_b"][1]], Q_UP * D ** -0.5, None, ALU.mult)\
                .then_inc(sem("qx_affine"), 1)
            dve.memset(nm_old[:, :], BIG)
            dve.memset(lsum[:, :], 0.0)
            for n in range(4):
                head_stats("qx", n, 4)
            for n in range(2):
                head_stats("k", n, 0)
            for n in range(4):
                sl = slice(4 * n, 4 * n + 4)
                dve.wait_ge(sem("qxhatT"), n + 1)
                dve.tensor_tensor(qx_hl[:, 1, sl, :], qx_full[:, sl, :], qx_hl[:, 0, sl, :], ALU.subtract).then_inc(sem("qx_lo"), 1)

            def wkv_low(g):
                dve.wait_ge(sem("wkv_hi"), g + 1)
                dve.scalar_tensor_tensor(out=w_hl[:, 1, :, g, :], in0=wkv_s[:, :, g * 2 * D:(g + 1) * 2 * D], scalar=W_UP,
                                         in1=w_hl[:, 0, :, g, :], op0=ALU.mult, op1=ALU.subtract).then_inc(sem("wkv_lo"), 1)

            for n in range(4):
                wkv_low(n)
                head_stats("q", n, 4)

            def own_max():
                dve.wait_ge(sem("own_scores_mm"), 1)
                link(dve.tensor_reduce(mx[:, :].rearrange("p (a b) -> p a b", a=4),
                                       ps[:, 4:8, :].rearrange("p a (b n) -> p a b n", b=4), AX, ALU.max))
                dve.tensor_scalar(nmx[:, :], mx[:, :], -D ** -0.5, None, ALU.mult).then_inc(sem("own_nmax"), 1)

            def unit_out(b, g, u):
                n, t0 = len(UNITS[u]), UNITS[u][0]
                bank = ps[:, KV + u % 2, :]
                dve.wait_ge(sem("v_hi"), count(b, g, 4, u + 1))
                for i in range(n):
                    ins = dve.bn_stats(kstat[:, u % 2, i, :], bank[:, i * 2 * D:i * 2 * D + D])
                ins.then_inc(sem("k_stat"), 1)
                dve.wait_ge(sem("k_stat"), count(b, g, 4, u + 1))
                dve.scalar_tensor_tensor(
                    out=vhl[:, g % 4, 1, t0 * P:(t0 + n) * P].rearrange("p (t d) -> p t d", d=D),
                    in0=bank[:, 0:n * 2 * D].rearrange("p (t k d) -> p t k d", k=2, d=D)[:, :, 1, :], scalar=V_UP / W_UP,
                    in1=vhl[:, g % 4, 0, t0 * P:(t0 + n) * P].rearrange("p (t d) -> p t d", d=D),
                    op0=ALU.mult, op1=ALU.subtract).then_inc(sem("v_lo"), 1)
                for i in range(n):
                    ins = dve.bn_aggr(kmv[:, u % 2, i, :], kstat[:, u % 2, i, :])
                ins.then_inc(sem("k_var"), 1)

            def unit_norm(b, g, u):
                dve.wait_ge(sem("k_rstd"), count(b, g, 4, u + 1))
                dve.wait_ge(sem("k_var"), count(b, g, 4, u + 1))
                for i, t in enumerate(UNITS[u]):
                    ins = dve.tensor_scalar(kn[:, g % 2, t * P:(t + 1) * P], ps[:, KV + u % 2, i * 2 * D:i * 2 * D + D],
                                            kmv[:, u % 2, i, 0:1], krstd[:, u % 2, i:i + 1], ALU.subtract, ALU.mult)
                ins.then_inc(sem("k_norm"), 1)

            def row_max(b, g, h):
                head = g * HPG + h
                dve.wait_ge(sem("scores_mm"), count(b, g, 2, h + 1))
                dve.tensor_reduce(bmax[:, head:head + 1], ps[:, SS:SS + 2, 0:HALF], mybir.AxisListType.XY, ALU.max)\
                    .then_inc(sem("block_max"), 1)
                dve.wait_ge(sem("block_max"), count(b, g, 2, h + 1))
                dve.tensor_scalar(nm_new[:, head:head + 1], bmax[:, head:head + 1], -1.0 / Q_UP, nm_old[:, head:head + 1],
                                  ALU.mult, ALU.min).then_inc(sem("nm_new"), 1)

            def p_low(b, g, h):
                for j, (t0, t1) in enumerate(TURNS):
                    dve.wait_ge(sem("p_hi"), count(b, g, 4, 2 * h + j + 1))
                    dve.scalar_tensor_tensor(out=prT[:, h, 1, t0 * P:t1 * P],
                                             in0=ps[:, TT + (2 * h + j) % 3, 0:(t1 - t0) * P], scalar=P_UP,
                                             in1=prT[:, h, 0, t0 * P:t1 * P], op0=ALU.mult, op1=ALU.subtract)\
                        .then_inc(sem("p_lo"), 1)

            def carry(b, g, h):
                head = g * HPG + h
                dve.wait_ge(sem("pv_mm"), count(b, g, 2, h + 1))
                dve.wait_ge(sem("alpha"), count(b, g, 2, h + 1))
                dve.scalar_tensor_tensor(out=acc[:, head, :], in0=acc[:, head, :], scalar=alpha[:, head:head + 1],
                                         in1=ps[:, OO, 0:D], op0=ALU.mult, op1=ALU.add).then_inc(sem("o_part"), 1)
                dve.scalar_tensor_tensor(out=lsum[:, head:head + 1], in0=lsum[:, head:head + 1], scalar=alpha[:, head:head + 1],
                                         in1=rsum[:, head:head + 1], op0=ALU.mult, op1=ALU.add)
                dve.wait_ge(sem("o_part"), count(b, g, 2, h + 1))
                dve.tensor_tensor(acc[:, head, :], ps[:, OO, D:2 * D], acc[:, head, :], ALU.add).then_inc(sem("o_done"), 1)
                dve.tensor_copy(nm_old[:, head:head + 1], nm_new[:, head:head + 1]).then_inc(sem("state"), 1)

            def x_scale(g):
                heads = slice(g * HPG, (g + 1) * HPG)
                dve.wait_ge(sem("state"), count(NBLK - 1, g, 2, 2))
                link(dve.reciprocal(rden[:, heads], lsum[:, heads]))
                for h in range(g * HPG, (g + 1) * HPG):
                    ins = dve.tensor_scalar(acc[:, h, :], acc[:, h, :], rden[:, h:h + 1], 1.0 / (V_UP * P_UP), ALU.mult, ALU.mult)
                ins.then_inc(sem("xout"), 1)

            def x_take(g):
                dve.wait_ge(sem("x_turn_mm"), g + 1)
                for h in range(HPG):
                    k = 4 * NC + NH + g * HPG + h
                    ins = dve.tensor_scalar(z_c[:, h, :], ps[:, TT + 1, h * T:(h + 1) * T], rcp_in[:, k:k + 1], FP8_MAX,
                                            ALU.mult, ALU.min)
                ins.then_inc(sem("x_taken"), 1)

            def own_round(n):
                y = coreq[:, 4 * n:4 * n + 4, :]
                link(dve.tensor_scalar(o_bf[:, :, :], y, FP8_MAX, -FP8_MAX, ALU.min, ALU.max))
                round_fp8(o_bf[:, :, :], y, o_c[:, :, :]).then_inc(sem("coreq"), 1)
                dve.wait_ge(sem("coreq"), n + 1)

            def x_round(g):
                heads = slice(g * HPG, (g + 1) * HPG)
                dve.wait_ge(sem("x_taken"), g + 1)
                link(dve.tensor_scalar(z_bf[:, :, :], z_c[:, :, :], -FP8_MAX, None, ALU.max))
                round_fp8(z_bf[:, :, :], acc[:, heads, :], z_c[:, :, :]).then_inc(sem("xoutq"), 1)

            def step(b, g, last):
                ahead = G - g if last else NBLK * G
                row_max(b, g, 1)
                if last and g:
                    x_scale(g - 1)
                p_low(b, g, 0)
                if ahead > 2:
                    unit_out(*on(b, g, 2), 1)
                    unit_norm(*on(b, g, 2), 1)
                    unit_out(*on(b, g, 2), 2)
                if last and g:
                    x_take(g - 1)
                if last and g == G - 2:
                    own_round(1)
                p_low(b, g, 1)
                if ahead > 2:
                    unit_norm(*on(b, g, 2), 2)
                carry(b, g, 0)
                if ahead > 2:
                    unit_out(*on(b, g, 2), 3)
                if ahead > 1:
                    row_max(*on(b, g, 1), 0)
                if ahead > 2:
                    unit_norm(*on(b, g, 2), 3)
                if last and g:
                    x_round(g - 1)
                if last and g == G - 3:
                    own_round(0)
                if last and g == G - 2:
                    own_round(2)
                    own_round(3)
                if ahead > 3:
                    unit_out(*on(b, g, 3), 0)
                carry(b, g, 1)
                if ahead > 3:
                    unit_norm(*on(b, g, 3), 0)

            def unit(b, g, u):
                unit_out(b, g, u)
                unit_norm(b, g, u)

            unit(0, 0, 0)
            wkv_low(4)
            unit(0, 0, 1)
            wkv_low(5)
            unit(0, 0, 2)
            own_max()
            unit(0, 0, 3)
            wkv_low(6)
            wkv_low(7)
            unit_out(0, 1, 0)
            dve.wait_ge(sem("own_probs"), NH)
            dve.reciprocal(rden[:, :], den[:, :]).then_inc(sem("own_rden"), 1)
            unit_norm(0, 1, 0)
            unit(0, 1, 1)
            unit(0, 1, 2)
            unit(0, 1, 3)
            row_max(0, 0, 0)
            unit(0, 2, 0)
            with dve.Fori(0, NBLK - 1) as b:
                for g in range(G):
                    step(b, g, False)
            for g in range(G):
                step(NBLK - 1, g, True)

            x_scale(G - 1)
            x_take(G - 1)
            x_round(G - 1)
            link(dve.tensor_tensor(pscale[:, :], scalar("proj_in"), scalar("proj_w"), ALU.mult))
            dve.wait_ge(sem("proj_mm"), 1)
            link(dve.scalar_tensor_tensor(out=xs[:, :], in0=ps[:, KV, :], scalar=pscale[:, 0:1], in1=xs[:, :], op0=ALU.mult, op1=ALU.add))

            norm_row("a", a_xn[:, :], xs[:, :], "a_xn")
            dve.wait_ge(sem("a_xT_mm"), 1)
            for c in range(NC):
                dve.tensor_scalar(a_xT[:, c, :], ps[:, 0, c * T:(c + 1) * T], col("ln_g2", c), col("ln_b2", c), ALU.mult, ALU.add)\
                    .then_inc(sem("a_xT"), 1)
            for k, (dst, mm, bias) in enumerate(((a_QT, "a_QT", "bq"), (a_KT, "a_KT", "bk"))):
                dve.wait_ge(sem(mm + "_mm"), 1)
                for m in range(NC):
                    dve.tensor_scalar(dst[:, m, :], ps[:, 1 + k, m * T:(m + 1) * T], col(bias, m), None, ALU.add)\
                        .then_inc(sem(mm), 1)
            dve.wait_ge(sem("a_V_mm"), 1)
            dve.tensor_tensor(a_V[:, :], ps[:, 3, :], rows[:, 0:C], ALU.add).then_inc(sem("a_V"), 1)
            dve.wait_ge(sem("causal"), 1)
            for j in range(4):
                dve.wait_ge(sem("a_scores_mm"), j + 1)
                strip = slice(4 * j, 4 * j + 4)
                link(dve.scalar_tensor_tensor(out=a_P[:, j, :, :], in0=ps[:, 4 + j, :].rearrange("p (m t) -> p m t", t=T),
                                              scalar=SD ** -0.5, in1=causal[:, :].unsqueeze(1).to_broadcast([P, NC, T]),
                                              op0=ALU.mult, op1=ALU.add))
                link(dve.tensor_reduce(mx[:, strip], a_P[:, j, :, :], AX, ALU.max))
                dve.tensor_scalar(nmx[:, strip], mx[:, strip], -1.0, None, ALU.mult).then_inc(sem("a_nmax"), 1)
            def up_low(it, k):
                it, k = (it, k) if k < SLOTS else (it + 1, k - SLOTS)
                dve.wait_ge(sem("up_hi"), it * SLOTS + (k + 1))
                dve.scalar_tensor_tensor(out=up_hl[:, k % 2, 1, :, :], in0=slots[k][0][:, :, :], scalar=W_UP,
                                         in1=up_hl[:, k % 2, 0, :, :], op0=ALU.mult, op1=ALU.subtract).then_inc(sem("up_lo"), 1)

            up_low(0, 0)
            up_low(0, 1)
            dve.wait_ge(sem("a_probs"), SH)
            link(dve.reciprocal(rden[:, :], den[:, :]))
            dve.wait_ge(sem("a_pv_mm"), 1)
            for k in range(SH):
                head = (k % 4) * 4 + k // 4
                ins = dve.tensor_scalar(a_o[:, head * SD:(head + 1) * SD], ps[:, 4, head * SD:(head + 1) * SD], rden[:, k:k + 1], None, ALU.mult)
            ins.then_inc(sem("a_o"), 1)
            dve.wait_ge(sem("a_oT_mm"), 1)
            dve.tensor_copy(a_oT[:, :, :], ps[:, 0, :].rearrange("p (c t) -> p c t", t=T)).then_inc(sem("a_oT"), 1)
            link(dve.tensor_tensor(xs[:, :], xs[:, :], rows[:, C:2 * C], ALU.add))
            dve.wait_ge(sem("a_out_mm"), 1)
            link(dve.tensor_tensor(xs[:, :], ps[:, 5, :], xs[:, :], ALU.add))

            dve.memset(zeros[:, :], 0.0).then_inc(sem("zeros"), 1)
            norm_row("e", a_xn[:, :], xs[:, :], "e_xn")
            dve.wait_ge(sem("e_xT_mm"), 1)
            dve.tensor_copy(a_xT[:, :, :], ps[:, 0, :].rearrange("p (c t) -> p c t", t=T)).then_inc(sem("e_xT"), 1)
            dve.wait_ge(sem("e_xT"), 1)
            link(dve.tensor_copy(e_xhl[:, 0, :, :], a_xT[:, :, :]))
            dve.tensor_tensor(e_xhl[:, 1, :, :], a_xT[:, :, :], e_xhl[:, 0, :, :], ALU.subtract).then_inc(sem("e_xT"), 1)
            dve.wait_ge(sem("logits_mm"), 1)
            link(dve.tensor_reduce(mx[:, 0:1], ps[:, 1, 0:E], AX, ALU.max))
            dve.tensor_scalar(nmx[:, 0:1], mx[:, 0:1], -1.0, None, ALU.mult).then_inc(sem("e_nmax"), 1)
            dve.wait_ge(sem("e_exp"), 1)
            link(dve.reciprocal(rden[:, 0:1], den[:, 0:1]))
            link(dve.tensor_scalar(gate[:, :], gate[:, :], rden[:, 0:1], None, ALU.mult))
            link(dve.max(top8[:, :], gate[:, :]))
            link(dve.match_replace(gate2[:, :], top8[:, :], gate[:, :], -1.0))
            link(dve.tensor_reduce(den[:, 0:1], top8[:, :], AX, ALU.add))
            link(dve.reciprocal(rden[:, 0:1], den[:, 0:1]))
            link(dve.tensor_scalar(rden[:, 0:1], rden[:, 0:1], 1.0 / W_UP, None, ALU.mult))
            link(dve.scalar_tensor_tensor(out=gate[:, :], in0=gate2[:, :], scalar=0.0, in1=gate[:, :], op0=ALU.is_lt, op1=ALU.mult))
            dve.tensor_scalar(gate[:, :], gate[:, :], rden[:, 0:1], None, ALU.mult).then_inc(sem("gate"), 1)
            dve.wait_ge(sem("gate"), 1)
            def experts(it, last):
                def turned(k):
                    dve.wait_ge(sem("hid_turn_mm"), it * SLOTS + (k + 1))
                    if k >= 2:
                        dve.wait_ge(sem("y_mm"), it * SLOTS + (k - 1))
                    dve.tensor_copy(hidT[:, k % 2, 0, :], ps[:, 4 + k % 2, 0:T]).then_inc(sem("hidT"), 1)
                    dve.tensor_copy(hidT[0:F - P, k % 2, 1, :], ps[0:F - P, 4 + k % 2, T:2 * T]).then_inc(sem("hidT"), 1)

                for k in range(SLOTS):
                    dve.wait_ge(sem("silu"), it * SLOTS + (k + 1))
                    if k >= 2:
                        dve.wait_ge(sem("hid_turn_mm"), it * SLOTS + (k - 1))
                    e = it * SLOTS + k
                    dve.scalar_tensor_tensor(out=hid[:, k % 2, :], in0=silu[:, k % 2, :],
                                             scalar=gate[:, e:e + 1] if last else gate[:, bass.ds(e, 1)],
                                             in1=ps[:, 2 + k % 2, F:2 * F], op0=ALU.mult, op1=ALU.mult).then_inc(sem("hid"), 1)
                    if k:
                        turned(k - 1)
                    if not last or k + 2 < SLOTS:
                        up_low(it, k + 2)
                turned(SLOTS - 1)

            with dve.Fori(0, E // SLOTS - 1) as it:
                experts(it, False)
            experts(E // SLOTS - 1, True)
            dve.wait_ge(sem("y_mm"), E)
            dve.tensor_tensor(xs[:, :], ps[:, 6, :], xs[:, :], ALU.add).then_inc(sem("final"), 1)


def kernel(**inputs):
    import numpy as np
    import concourse.bacc as bacc
    from concourse.bass_utils import run_bass_kernel_spmd

    a = {k: np.asarray(v) for k, v in inputs.items()}

    def columns(v):
        return v.reshape(-1, P).T

    xa = "L0_xattn_"
    parts = {"q_in": a[xa + "q_in_scale"], "qx_in": a[xa + "qx_in_scale"], "k_in": a[xa + "k_in_scale"],
             "v_in": a[xa + "v_in_scale"], "smooth": a[xa + "proj_smooth"], "ln_w": a[xa + "ln_w"], "ln_b": a[xa + "ln_b"],
             "ln_g2": a["L0_attn_ln_g"], "ln_b2": a["L0_attn_ln_b"], "bq": a["L0_attn_bq"], "bk": a["L0_attn_bk"]}
    for n in ("qln_w", "qln_b", "kln_w", "kln_b", "qxln_w", "qxln_b", "kxln_w", "kxln_b"):
        parts[n] = a[xa + n]
    cols = np.concatenate([columns(parts[n]) for n in COLS], axis=1)
    scalars = [a[xa + n].reshape(1) for n in ("wq_scale", "wqx_scale", "wk_scale", "wv_scale", "proj_w_scale", "proj_in_scale")]
    rows = np.concatenate([a["L0_attn_bv"], a["L0_attn_bo"], *scalars])
    wkv = a[xa + "w_kv_x"].reshape(2, G, D, C).transpose(3, 1, 0, 2).reshape(C, 2 * G * D)
    arrays = {
        "x": a["x"][0], "ctxT": a["ctx_2048"][0].T, "wqT": a[xa + "wq"].T, "wqxT": a[xa + "wqx"].T, "wkT": a[xa + "wk"].T,
        "wvT": a[xa + "wv"].T, "wkvT": wkv, "wprojT": a[xa + "wproj"].T, "cols": cols, "rows": rows,
        "Wq": a["L0_attn_Wq"], "Wk": a["L0_attn_Wk"], "Wv": a["L0_attn_Wv"], "Wo": a["L0_attn_Wo"], "wgT": a["L0_ffn_wg"].T,
        "w1v1": np.concatenate([a["L0_ffn_w1"], a["L0_ffn_v1"]], axis=2), "w2": a["L0_ffn_w2"],
    }
    arrays = {f"in_{k}": np.ascontiguousarray(v) for k, v in arrays.items()}
    nc = bacc.Bacc("TRN2", target_bir_lowering=False, num_devices=1)
    args = [nc.dram_tensor(k, v.shape, mybir.dt.from_np(v.dtype), kind="ExternalInput").ap() for k, v in arrays.items()]
    args.append(nc.dram_tensor("out_0", (T, C), F32, kind="ExternalOutput").ap())
    build(nc, *args)
    r = run_bass_kernel_spmd(nc, [arrays], core_ids=[0])
    return r.results[0]["out_0"].reshape(1, T, C)
```
